# Optimizing a Trainium2 kernel written in Bass

```python
import numpy as np
import jax
import jax.numpy as jnp

def _softmax(x, axis=-1):
    return jax.nn.softmax(x, axis=axis)

def _gelu(x):
    return jax.nn.gelu(x, approximate=True)

def _silu(x):
    return jax.nn.silu(x)

def _sigmoid(x):
    return jax.nn.sigmoid(x)

def _layernorm(x, axis=-1, eps=1e-05):
    m = jnp.mean(x, axis=axis, keepdims=True)
    v = jnp.var(x, axis=axis, keepdims=True)
    return (x - m) / jnp.sqrt(v + eps)

def _scatter_add(tgt, idx, src, axis=0):
    return tgt.at[idx].add(src)

def _segment_sum(src, seg, n):
    return jax.ops.segment_sum(src, seg, n)
kernel_name = 'mk_dlrm_tower_d1_rec_r8_184d38'

def setup_inputs(seed: int=0):
    np.random.seed(seed)
    _w = jnp.asarray

    def _rec_inputs():
        import jax
        import jax.numpy as jnp
        _tk = jax.random.key(seed)
        dense_ctx = jax.random.normal(jax.random.fold_in(_tk, 190), (1024, 16), jnp.float32)
        ids = jnp.stack([jax.random.randint(jax.random.fold_in(_tk, 200 + f), (1024,), 0, v, jnp.int32) for f, v in enumerate([1000, 1000, 1250, 125000, 1000, 125000, 12500, 1250, 125000, 1000, 1250, 12500, 12500, 125000, 12500, 12500, 1250, 1250, 1000, 1250, 12500, 12500, 1250, 12500, 1250, 1000, 1000, 125000, 125000, 125000, 1000, 12500, 125000, 12500, 1250, 125000, 12500, 125000, 1250])], axis=1)
        tbl_0 = 0.05 * jax.random.normal(jax.random.fold_in(_tk, 500 + 0), (1000, 16), jnp.float32)
        tbl_1 = 0.05 * jax.random.normal(jax.random.fold_in(_tk, 500 + 1), (1000, 16), jnp.float32)
        tbl_2 = 0.05 * jax.random.normal(jax.random.fold_in(_tk, 500 + 2), (1250, 16), jnp.float32)
        tbl_3 = 0.05 * jax.random.normal(jax.random.fold_in(_tk, 500 + 3), (125000, 16), jnp.float32)
        tbl_4 = 0.05 * jax.random.normal(jax.random.fold_in(_tk, 500 + 4), (1000, 16), jnp.float32)
        tbl_5 = 0.05 * jax.random.normal(jax.random.fold_in(_tk, 500 + 5), (125000, 16), jnp.float32)
        tbl_6 = 0.05 * jax.random.normal(jax.random.fold_in(_tk, 500 + 6), (12500, 16), jnp.float32)
        tbl_7 = 0.05 * jax.random.normal(jax.random.fold_in(_tk, 500 + 7), (1250, 16), jnp.float32)
        tbl_8 = 0.05 * jax.random.normal(jax.random.fold_in(_tk, 500 + 8), (125000, 16), jnp.float32)
        tbl_9 = 0.05 * jax.random.normal(jax.random.fold_in(_tk, 500 + 9), (1000, 16), jnp.float32)
        tbl_10 = 0.05 * jax.random.normal(jax.random.fold_in(_tk, 500 + 10), (1250, 16), jnp.float32)
        tbl_11 = 0.05 * jax.random.normal(jax.random.fold_in(_tk, 500 + 11), (12500, 16), jnp.float32)
        tbl_12 = 0.05 * jax.random.normal(jax.random.fold_in(_tk, 500 + 12), (12500, 16), jnp.float32)
        tbl_13 = 0.05 * jax.random.normal(jax.random.fold_in(_tk, 500 + 13), (125000, 16), jnp.float32)
        tbl_14 = 0.05 * jax.random.normal(jax.random.fold_in(_tk, 500 + 14), (12500, 16), jnp.float32)
        tbl_15 = 0.05 * jax.random.normal(jax.random.fold_in(_tk, 500 + 15), (12500, 16), jnp.float32)
        tbl_16 = 0.05 * jax.random.normal(jax.random.fold_in(_tk, 500 + 16), (1250, 16), jnp.float32)
        tbl_17 = 0.05 * jax.random.normal(jax.random.fold_in(_tk, 500 + 17), (1250, 16), jnp.float32)
        tbl_18 = 0.05 * jax.random.normal(jax.random.fold_in(_tk, 500 + 18), (1000, 16), jnp.float32)
        tbl_19 = 0.05 * jax.random.normal(jax.random.fold_in(_tk, 500 + 19), (1250, 16), jnp.float32)
        tbl_20 = 0.05 * jax.random.normal(jax.random.fold_in(_tk, 500 + 20), (12500, 16), jnp.float32)
        tbl_21 = 0.05 * jax.random.normal(jax.random.fold_in(_tk, 500 + 21), (12500, 16), jnp.float32)
        tbl_22 = 0.05 * jax.random.normal(jax.random.fold_in(_tk, 500 + 22), (1250, 16), jnp.float32)
        tbl_23 = 0.05 * jax.random.normal(jax.random.fold_in(_tk, 500 + 23), (12500, 16), jnp.float32)
        tbl_24 = 0.05 * jax.random.normal(jax.random.fold_in(_tk, 500 + 24), (1250, 16), jnp.float32)
        tbl_25 = 0.05 * jax.random.normal(jax.random.fold_in(_tk, 500 + 25), (1000, 16), jnp.float32)
        tbl_26 = 0.05 * jax.random.normal(jax.random.fold_in(_tk, 500 + 26), (1000, 16), jnp.float32)
        tbl_27 = 0.05 * jax.random.normal(jax.random.fold_in(_tk, 500 + 27), (125000, 16), jnp.float32)
        tbl_28 = 0.05 * jax.random.normal(jax.random.fold_in(_tk, 500 + 28), (125000, 16), jnp.float32)
        tbl_29 = 0.05 * jax.random.normal(jax.random.fold_in(_tk, 500 + 29), (125000, 16), jnp.float32)
        tbl_30 = 0.05 * jax.random.normal(jax.random.fold_in(_tk, 500 + 30), (1000, 16), jnp.float32)
        tbl_31 = 0.05 * jax.random.normal(jax.random.fold_in(_tk, 500 + 31), (12500, 16), jnp.float32)
        tbl_32 = 0.05 * jax.random.normal(jax.random.fold_in(_tk, 500 + 32), (125000, 16), jnp.float32)
        tbl_33 = 0.05 * jax.random.normal(jax.random.fold_in(_tk, 500 + 33), (12500, 16), jnp.float32)
        tbl_34 = 0.05 * jax.random.normal(jax.random.fold_in(_tk, 500 + 34), (1250, 16), jnp.float32)
        tbl_35 = 0.05 * jax.random.normal(jax.random.fold_in(_tk, 500 + 35), (125000, 16), jnp.float32)
        tbl_36 = 0.05 * jax.random.normal(jax.random.fold_in(_tk, 500 + 36), (12500, 16), jnp.float32)
        tbl_37 = 0.05 * jax.random.normal(jax.random.fold_in(_tk, 500 + 37), (125000, 16), jnp.float32)
        tbl_38 = 0.05 * jax.random.normal(jax.random.fold_in(_tk, 500 + 38), (1250, 16), jnp.float32)
        _rk = jax.random.fold_in(_tk, 7)
        W_top1 = 0.0606339 * jax.random.normal(jax.random.fold_in(_tk, 801), (272, 512), jnp.float32)
        W_top2 = 0.0441942 * jax.random.normal(jax.random.fold_in(_tk, 802), (512, 256), jnp.float32)
        W_top3 = 0.0625 * jax.random.normal(jax.random.fold_in(_tk, 803), (256, 1), jnp.float32)
        b_top1 = jnp.zeros((512,), jnp.float32)
        b_top2 = jnp.zeros((256,), jnp.float32)
        return (dense_ctx, ids, tbl_0, tbl_1, tbl_2, tbl_3, tbl_4, tbl_5, tbl_6, tbl_7, tbl_8, tbl_9, tbl_10, tbl_11, tbl_12, tbl_13, tbl_14, tbl_15, tbl_16, tbl_17, tbl_18, tbl_19, tbl_20, tbl_21, tbl_22, tbl_23, tbl_24, tbl_25, tbl_26, tbl_27, tbl_28, tbl_29, tbl_30, tbl_31, tbl_32, tbl_33, tbl_34, tbl_35, tbl_36, tbl_37, tbl_38, W_top1, b_top1, W_top2, b_top2, W_top3)
    dense_ctx, ids, tbl_0, tbl_1, tbl_2, tbl_3, tbl_4, tbl_5, tbl_6, tbl_7, tbl_8, tbl_9, tbl_10, tbl_11, tbl_12, tbl_13, tbl_14, tbl_15, tbl_16, tbl_17, tbl_18, tbl_19, tbl_20, tbl_21, tbl_22, tbl_23, tbl_24, tbl_25, tbl_26, tbl_27, tbl_28, tbl_29, tbl_30, tbl_31, tbl_32, tbl_33, tbl_34, tbl_35, tbl_36, tbl_37, tbl_38, W_top1, b_top1, W_top2, b_top2, W_top3 = _rec_inputs()

    def _L0_rec_setup():
        import jax, jax.numpy as jnp
        import numpy as np
        LAYER_SIZES = [128, 128, 128]
        F0 = 39
        D = 16
        B = 256
        key = jax.random.key(seed)
        ks = jax.random.split(key, 4)
        field_nums = [F0, LAYER_SIZES[0] // 2, LAYER_SIZES[1] // 2]
        x = jax.random.normal(ks[0], (B, F0, D), dtype=jnp.float32)
        W0 = jax.random.normal(ks[1], (F0 * field_nums[0], LAYER_SIZES[0]), dtype=jnp.float32) * 0.05
        W1 = jax.random.normal(ks[2], (F0 * field_nums[1], LAYER_SIZES[1]), dtype=jnp.float32) * 0.05
        W2 = jax.random.normal(ks[3], (F0 * field_nums[2], LAYER_SIZES[2]), dtype=jnp.float32) * 0.05
        b0 = jnp.zeros((LAYER_SIZES[0],), jnp.float32)
        b1 = jnp.zeros((LAYER_SIZES[1],), jnp.float32)
        b2 = jnp.zeros((LAYER_SIZES[2],), jnp.float32)
        return {'x': x, 'W0': W0, 'W1': W1, 'W2': W2, 'b0': b0, 'b1': b1, 'b2': b2}
    _L0_rec_all = _L0_rec_setup()
    _L0_rec_in = {k: v for k, v in _L0_rec_all.items() if k in ('W0', 'W1', 'W2', 'b0', 'b1', 'b2')}
    del _L0_rec_all
    return {'dense_ctx': dense_ctx, 'ids': ids, 'tbl_0': tbl_0, 'tbl_1': tbl_1, 'tbl_2': tbl_2, 'tbl_3': tbl_3, 'tbl_4': tbl_4, 'tbl_5': tbl_5, 'tbl_6': tbl_6, 'tbl_7': tbl_7, 'tbl_8': tbl_8, 'tbl_9': tbl_9, 'tbl_10': tbl_10, 'tbl_11': tbl_11, 'tbl_12': tbl_12, 'tbl_13': tbl_13, 'tbl_14': tbl_14, 'tbl_15': tbl_15, 'tbl_16': tbl_16, 'tbl_17': tbl_17, 'tbl_18': tbl_18, 'tbl_19': tbl_19, 'tbl_20': tbl_20, 'tbl_21': tbl_21, 'tbl_22': tbl_22, 'tbl_23': tbl_23, 'tbl_24': tbl_24, 'tbl_25': tbl_25, 'tbl_26': tbl_26, 'tbl_27': tbl_27, 'tbl_28': tbl_28, 'tbl_29': tbl_29, 'tbl_30': tbl_30, 'tbl_31': tbl_31, 'tbl_32': tbl_32, 'tbl_33': tbl_33, 'tbl_34': tbl_34, 'tbl_35': tbl_35, 'tbl_36': tbl_36, 'tbl_37': tbl_37, 'tbl_38': tbl_38, 'W_top1': W_top1, 'b_top1': b_top1, 'W_top2': W_top2, 'b_top2': b_top2, 'W_top3': W_top3, 'L0_rec_W0': _L0_rec_in['W0'], 'L0_rec_W1': _L0_rec_in['W1'], 'L0_rec_W2': _L0_rec_in['W2'], 'L0_rec_b0': _L0_rec_in['b0'], 'L0_rec_b1': _L0_rec_in['b1'], 'L0_rec_b2': _L0_rec_in['b2']}

def reference(dense_ctx, ids, tbl_0, tbl_1, tbl_2, tbl_3, tbl_4, tbl_5, tbl_6, tbl_7, tbl_8, tbl_9, tbl_10, tbl_11, tbl_12, tbl_13, tbl_14, tbl_15, tbl_16, tbl_17, tbl_18, tbl_19, tbl_20, tbl_21, tbl_22, tbl_23, tbl_24, tbl_25, tbl_26, tbl_27, tbl_28, tbl_29, tbl_30, tbl_31, tbl_32, tbl_33, tbl_34, tbl_35, tbl_36, tbl_37, tbl_38, W_top1, b_top1, W_top2, b_top2, W_top3, L0_rec_W0, L0_rec_W1, L0_rec_W2, L0_rec_b0, L0_rec_b1, L0_rec_b2):
    import jax
    import jax.numpy as jnp

    def _L0_rec_ref(x, W0, W1, W2, b0, b1, b2):
        import jax, jax.numpy as jnp
        import numpy as np
        LAYER_SIZES = [128, 128, 128]
        F0 = 39
        D = 16
        B = 256
        Ws = [W0, W1, W2]
        bs = [b0, b1, b2]
        h = x
        outs = []
        n_layers = len(LAYER_SIZES)
        for i, S in enumerate(LAYER_SIZES):
            Fk = h.shape[1]
            Wr = Ws[i].reshape(F0, Fk, S)
            out = jax.nn.relu(jnp.einsum('bfd,bgd,fgs->bsd', x, h, Wr) + bs[i][None, :, None])
            if i != n_layers - 1:
                h, direct = (out[:, :S // 2], out[:, S // 2:])
            else:
                direct = out
            outs.append(direct)
        result = jnp.concatenate(outs, axis=1)
        return jnp.sum(result, axis=-1)
    e = jnp.stack([tbl_0[ids[:, 0]], tbl_1[ids[:, 1]], tbl_2[ids[:, 2]], tbl_3[ids[:, 3]], tbl_4[ids[:, 4]], tbl_5[ids[:, 5]], tbl_6[ids[:, 6]], tbl_7[ids[:, 7]], tbl_8[ids[:, 8]], tbl_9[ids[:, 9]], tbl_10[ids[:, 10]], tbl_11[ids[:, 11]], tbl_12[ids[:, 12]], tbl_13[ids[:, 13]], tbl_14[ids[:, 14]], tbl_15[ids[:, 15]], tbl_16[ids[:, 16]], tbl_17[ids[:, 17]], tbl_18[ids[:, 18]], tbl_19[ids[:, 19]], tbl_20[ids[:, 20]], tbl_21[ids[:, 21]], tbl_22[ids[:, 22]], tbl_23[ids[:, 23]], tbl_24[ids[:, 24]], tbl_25[ids[:, 25]], tbl_26[ids[:, 26]], tbl_27[ids[:, 27]], tbl_28[ids[:, 28]], tbl_29[ids[:, 29]], tbl_30[ids[:, 30]], tbl_31[ids[:, 31]], tbl_32[ids[:, 32]], tbl_33[ids[:, 33]], tbl_34[ids[:, 34]], tbl_35[ids[:, 35]], tbl_36[ids[:, 36]], tbl_37[ids[:, 37]], tbl_38[ids[:, 38]]], axis=1)
    z = _L0_rec_ref(e, L0_rec_W0, L0_rec_W1, L0_rec_W2, L0_rec_b0, L0_rec_b1, L0_rec_b2)
    z = z.reshape(z.shape[0], -1)
    h = jnp.concatenate([z, dense_ctx], axis=1)
    h = jnp.maximum(h @ W_top1 + b_top1, 0.0)
    h = jnp.maximum(h @ W_top2 + b_top2, 0.0)
    y = h @ W_top3
    return y

_drawn_inputs = setup_inputs


def setup_inputs(seed=0):
    import zlib

    import numpy as np

    out = dict(_drawn_inputs(seed))
    spreads = {'b_top1': (0.0, 0.8),
     'b_top2': (0.0, 0.8),
     'L0_rec_b0': (0.0, 0.316),
     'L0_rec_b1': (0.0, 0.461),
     'L0_rec_b2': (0.0, 0.274)}
    factors = {'tbl_0': 8.0,
     'tbl_1': 8.0,
     'tbl_2': 8.0,
     'tbl_3': 8.0,
     'tbl_4': 8.0,
     'tbl_5': 8.0,
     'tbl_6': 8.0,
     'tbl_7': 8.0,
     'tbl_8': 8.0,
     'tbl_9': 8.0,
     'tbl_10': 8.0,
     'tbl_11': 8.0,
     'tbl_12': 8.0,
     'tbl_13': 8.0,
     'tbl_14': 8.0,
     'tbl_15': 8.0,
     'tbl_16': 8.0,
     'tbl_17': 8.0,
     'tbl_18': 8.0,
     'tbl_19': 8.0,
     'tbl_20': 8.0,
     'tbl_21': 8.0,
     'tbl_22': 7.292,
     'tbl_23': 8.0,
     'tbl_24': 8.0,
     'tbl_25': 8.0,
     'tbl_26': 7.364,
     'tbl_27': 8.0,
     'tbl_28': 8.0,
     'tbl_29': 8.0,
     'tbl_30': 8.0,
     'tbl_31': 7.537,
     'tbl_32': 8.0,
     'tbl_33': 8.0,
     'tbl_34': 8.0,
     'tbl_35': 8.0,
     'tbl_36': 8.0,
     'tbl_37': 8.0,
     'tbl_38': 8.0,
     'L0_rec_W0': 6.481,
     'L0_rec_W1': 3.302,
     'dense_ctx': 5.762}
    for name, (base, spread) in spreads.items():
        noise = np.random.default_rng([zlib.crc32(name.encode()), seed]).standard_normal(out[name].shape)
        drawn = base * np.exp(spread * noise) if base else spread * noise
        out[name] = jnp.asarray(drawn.astype(out[name].dtype))
    for name, factor in factors.items():
        out[name] = (out[name] * factor).astype(out[name].dtype)
    return out
```

```python
from contextlib import ExitStack

import numpy as np
import concourse.bass as bass
from concourse import mybir

F32 = mybir.dt.float32
I32 = mybir.dt.int32
U32 = mybir.dt.uint32
ALU = mybir.AluOpType
ACT = mybir.ActivationFunctionType
AX = mybir.AxisListType

P = 128
FIELDS = 39
FP = 40
D = 16
XGF = 72
BATCH = 1024
GROUPS = BATCH // P
K = 4
DK = D // K
N = DK * P
S = 128
H = 64
QI, QN = 5, 8
RJ, RN = 4, 16
PAIR_TILES = QI * RJ
ROT, ROWS0 = 3, 3 * FP
FAR = 23
TILES0 = (4, 3)
DOUBLE = 2 * FP
RING = 4
SLOTS0 = 2 * K
SLOTS12 = QI * K
SLOTS = SLOTS0 + 2 * SLOTS12
ACCS = 3 * K
M1, M2 = 512, 256
T1, T2 = M1 // P, M2 // P
DENSE = 16


def build(nc, io, tables):
    ctx = ExitStack()
    with ctx:
        def sb(name, shape, dt=F32):
            return ctx.enter_context(nc.sbuf_tensor(name, shape, dt))

        def ps(name, shape):
            return ctx.enter_context(nc.psum_tensor(name, shape, F32))

        def sem(name):
            return ctx.enter_context(nc.semaphore(name))

        x_rows = nc.dram_tensor("x_rows", (GROUPS, K, DOUBLE, N), F32).ap()
        h_rows = [nc.dram_tensor(f"h{n}_rows", (GROUPS, K, H, N), F32).ap() for n in (1, 2)]

        w0 = sb("w0", [ROWS0, sum(TILES0), S])
        w12 = [sb(f"w{n}", [P, PAIR_TILES, S]) for n in (1, 2)]
        wt1 = sb("wt1", [P, 2, M1])
        wt1d = sb("wt1d", [DENSE, M1])
        wt2 = sb("wt2", [P, T1, M2])
        wt3 = sb("wt3", [P, T2])
        bias = sb("bias", [P, 3])
        bt1 = sb("bt1", [P, T1])
        bt2 = sb("bt2", [P, T2])
        dense_y = sb("dense_y", [33, BATCH])
        dense = dense_y[0:DENSE, :]
        ident = sb("ident", [P, P])
        ids = sb("ids", [P, FIELDS], I32)
        xg = sb("xg", [P, XGF, D])
        xt = sb("xt", [FP, K, N])
        lx = sb("lx", [ROWS0, 2, 2, N])
        ly = sb("ly", [ROWS0, 2, 4, N])
        xa = sb("xa", [P, K, QI, N])
        hb = sb("hb", [P, K, RJ, N])
        z = sb("z", [P, RING, 4, N])
        hst = sb("hst", [P, K, N])
        r01 = sb("r01", [P, K, N])
        r2 = sb("r2", [P, K, N])
        zs01 = sb("zs01", [P, P])
        zs2 = sb("zs2", [P, P])
        h1 = sb("h1", [P, T1, P])
        h2 = sb("h2", [P, T2, P])
        y = dense_y[32:33, :]

        acc = [ps(f"acc{k}", [P, N]) for k in range(K)]
        xt_ps = [ps(f"xt_ps{i}", [P, N]) for i in range(2)]
        h1_ps = ps("h1_ps", [P, T1, P])
        h2_ps = ps("h2_ps", [P, 4, P])

        w0_loaded = sem("w0_loaded")
        w_loaded = [sem(f"w{n}_loaded") for n in (1, 2)]
        small_loaded = sem("small_loaded")
        w0_folded = sem("w0_folded")
        ident_zeroed = sem("ident_zeroed")
        pad_zeroed = sem("pad_zeroed")
        ident_made = sem("ident_made")
        ids_loaded = sem("ids_loaded")
        gathered = sem("gathered")
        x_transposed = sem("x_transposed")
        xt_copied = sem("xt_copied")
        x_stored = sem("x_stored")
        l0_loaded = [sem(f"l0_loaded{i}") for i in range(2)]
        xa_loaded = [sem(f"xa_loaded{k}") for k in range(K)]
        hb_loaded = [sem(f"hb_loaded{k}") for k in range(K)]
        z_ready = sem("z_ready")
        z_used = sem("z_used")
        acc_copied = sem("acc_copied")
        h_copied = sem("h_copied")
        h_stored = [[sem(f"h{n}_stored{k}") for k in range(K)] for n in (1, 2)]
        r01_summed = sem("r01_summed")
        r2_summed = sem("r2_summed")
        mlp1_done = sem("mlp1_done")
        h1_ready = sem("h1_ready")
        mlp2_done = sem("mlp2_done")
        h2_ready = sem("h2_ready")
        mlp3_done = sem("mlp3_done")
        y_ready = sem("y_ready")
        y_stored = sem("y_stored")

        block = ctx.enter_context(nc.Block())

        def slot0(g, k, u):
            return SLOTS * g + 2 * k + u

        def slot12(g, layer, k, i):
            return SLOTS * g + SLOTS0 + SLOTS12 * (layer - 1) + QI * k + i

        def acc_no(g, layer, k):
            return ACCS * g + K * layer + k

        def window(view, steps):
            return bass.AP(view.tensor, view.offset, steps)

        SMALL = [(wt1, "wt1"), (wt1d, "wt1d"), (wt2, "wt2"), (wt3, "wt3"), (bias, "bias"), (bt1, "bt1"),
                 (bt2, "bt2"), (dense, "dense")]

        @block.sync
        def _(sp):
            sp.dma_start(w0[:], io["w0a"]).then_inc(w0_loaded, 16)
            sp.dma_start(z[0:ROWS0, 0, 0:2, :].rearrange("p a n -> p (a n)")[:, 0:7 * S],
                         io["w0b"].rearrange("p t s -> p (t s)")).then_inc(w0_loaded, 16)
            for dst, name in SMALL:
                sp.dma_start(dst[:], io[name]).then_inc(small_loaded, 16)
            for n in range(2):
                sp.dma_start(w12[n][:], io[f"w{n + 1}"]).then_inc(w_loaded[n], 16)

            def load_l0(g, k):
                rows = x_rows[g, k]
                for c in range(ROT):
                    sp.dma_start(lx[FP * c:FP * (c + 1), k % 2],
                                 window(rows, [[N, FP], [FAR * N, 2], [1, N]])).then_inc(l0_loaded[k % 2], 16)
                    sp.dma_start(ly[FP * c:FP * (c + 1), k % 2],
                                 window(x_rows[g, k, c:c + 1], [[N, FP], [ROT * N, 4], [1, N]])
                                 ).then_inc(l0_loaded[k % 2], 16)

            def load_xa(g, k):
                sp.dma_start(xa[:, k], window(x_rows[g, k], [[0, RN], [QI * N, QN], [1, QI * N]])
                             ).then_inc(xa_loaded[k], 16)

            def load_hb(g, layer, k):
                sp.wait_ge(h_stored[layer - 1][k], 16 * (g + 1))
                sp.dma_start(hb[:, k], window(h_rows[layer - 1][g, k], [[RJ * N, RN], [0, QN], [1, RJ * N]])
                             ).then_inc(hb_loaded[k], 16)

            sp.wait_ge(x_stored, 32)
            load_l0(0, 0)
            load_l0(0, 1)
            load_xa(0, 0)
            sp.wait_ge(z_ready, slot0(0, 0, 1) + 1)
            load_l0(0, 2)
            load_hb(0, 1, 0)
            sp.wait_ge(z_ready, slot0(0, 1, 1) + 1)
            load_l0(0, 3)
            for k in range(1, K):
                load_xa(0, k)
                load_hb(0, 1, k)

            with sp.Fori(0, GROUPS - 1) as g:
                for k in range(K):
                    sp.wait_ge(z_ready, slot12(g, 1, k, QI - 1) + 1)
                    load_hb(g, 2, k)
                sp.wait_ge(x_stored, 32 * (g + 2))
                load_l0(g + 1, 0)
                load_l0(g + 1, 1)
                for k in range(K):
                    sp.wait_ge(z_ready, slot12(g, 2, k, QI - 1) + 1)
                    load_xa(g + 1, k)
                for k in range(K):
                    if k < 2:
                        sp.wait_ge(z_ready, slot0(g + 1, k, 1) + 1)
                        load_l0(g + 1, k + 2)
                    load_hb(g + 1, 1, k)
            for k in range(K):
                sp.wait_ge(z_ready, slot12(GROUPS - 1, 1, k, QI - 1) + 1)
                load_hb(GROUPS - 1, 2, k)

        @block.gpsimd
        def _(pool):
            def load_ids(g):
                pool.dma_start(ids[:], io["ids"][g]).then_inc(ids_loaded, 16)

            def gather():
                for f in range(FIELDS):
                    nc.gpsimd.indirect_dma_start(
                        xg[:, f, :], None, tables[f],
                        bass.IndirectOffsetOnAxis(ids[:, f:f + 1].bitcast(U32), 0)).then_inc(gathered, 16)

            load_ids(0)
            nc.gpsimd.memset(ident[:], 0.0).then_inc(ident_zeroed, 1)
            nc.gpsimd.memset(xg[:, FIELDS:, :], 0.0).then_inc(pad_zeroed, 1)
            pool.wait_ge(ident_zeroed, 1)
            nc.gpsimd.affine_select(out=ident[:], in_=ident[:], compare_op=ALU.not_equal, fill=1.0, base=0,
                                    pattern=[[-1, P]], channel_multiplier=1).then_inc(ident_made, 1)
            pool.wait_ge(ids_loaded, 16)
            with pool.Fori(0, GROUPS - 1) as g:
                gather()
                pool.wait_ge(gathered, 16 * FIELDS * (g + 1))
                load_ids(g + 1)
                pool.wait_ge(x_transposed, K * (g + 1))
                pool.wait_ge(ids_loaded, 16 * (g + 2))
            gather()

        @block.vector
        def _(dve):
            dve.wait_ge(w0_loaded, 32)
            nc.vector.tensor_tensor(w0[:].rearrange("p t s -> p (t s)"), w0[:].rearrange("p t s -> p (t s)"),
                                    z[0:ROWS0, 0, 0:2, :].rearrange("p a n -> p (a n)")[:, 0:7 * S],
                                    ALU.add).then_inc(w0_folded, 1)
            dve.wait_ge(w0_folded, 1)

            def free_slot(n, static=None):
                if static is None or static >= RING:
                    dve.wait_ge(z_used, n - RING + 1)

            def products0(g, k, first=False):
                dve.wait_ge(l0_loaded[k % 2], 16 * 2 * ROT * (2 * g + k // 2 + 1))
                for u, tiles in enumerate(TILES0):
                    n = slot0(g, k, u)
                    free_slot(n, slot0(0, k, u) if first else None)
                    nc.vector.tensor_tensor(
                        z[0:ROWS0, (2 * k + u) % RING, 0:tiles, :],
                        lx[:, k % 2, u:u + 1, :].to_broadcast([ROWS0, tiles, N]),
                        ly[:, k % 2, 4 - tiles:4, :], ALU.mult).then_inc(z_ready, 1)

            def products12(g, layer, k):
                dve.wait_ge(xa_loaded[k], 16 * (g + 1))
                dve.wait_ge(hb_loaded[k], 16 * (2 * g + layer))
                for i in range(QI):
                    free_slot(slot12(g, layer, k, i))
                    nc.vector.tensor_tensor(
                        z[:, slot12(0, layer, k, i) % RING],
                        xa[:, k, i:i + 1, :].to_broadcast([P, RJ, N]), hb[:, k], ALU.mult).then_inc(z_ready, 1)

            def sum_positions(out, r, done):
                nc.vector.tensor_reduce(out[:], r[:].rearrange("p k (d b) -> p b (k d)", b=P), AX.X,
                                        ALU.add).then_inc(done, 1)

            def sum01(g):
                dve.wait_ge(acc_copied, acc_no(g, 1, K - 1) + 1)
                sum_positions(zs01, r01, r01_summed)

            def sum2(g):
                dve.wait_ge(acc_copied, acc_no(g, 2, K - 1) + 1)
                sum_positions(zs2, r2, r2_summed)

            def group(g):
                for k in range(K):
                    products12(g, 1, k)
                for k in range(K):
                    products12(g, 2, k)
                    if k == 1:
                        sum01(g)

            for k in range(K):
                products0(0, k, first=True)
            with dve.Fori(0, GROUPS - 1) as g:
                group(g)
                for k in range(K):
                    products0(g + 1, k)
                    if k == 1:
                        sum2(g)
            group(GROUPS - 1)
            sum2(GROUPS - 1)

        @block.tensor
        def _(pe):
            def transposes(g, first=False):
                pe.wait_ge(gathered, 16 * FIELDS * (g + 1))
                for k in range(K):
                    if not (first and k < 2):
                        pe.wait_ge(xt_copied, K * g + k - 1)
                    for d in range(DK):
                        last = nc.tensor.transpose(xt_ps[k % 2][0:XGF, d * P:(d + 1) * P],
                                                   xg[:, :, k * DK + d], ident[:])
                    last.then_inc(x_transposed, 1)

            def open_acc(g, layer, k, first=False):
                if not first:
                    pe.wait_ge(acc_copied, acc_no(g, layer, k) - K + 1)

            def layer0(g, k, first=False):
                open_acc(g, 0, k, first)
                t = 0
                for u, tiles in enumerate(TILES0):
                    pe.wait_ge(z_ready, slot0(g, k, u) + 1)
                    for v in range(tiles):
                        last = nc.tensor.matmul(acc[k][:], w0[:, t, :], z[0:ROWS0, (2 * k + u) % RING, v, :],
                                                start=(t == 0), stop=(t == sum(TILES0) - 1))
                        t += 1
                    last.then_inc(z_used, 1)

            def layer12(g, layer, k):
                open_acc(g, layer, k)
                for i in range(QI):
                    pe.wait_ge(z_ready, slot12(g, layer, k, i) + 1)
                    for j in range(RJ):
                        t = RJ * i + j
                        last = nc.tensor.matmul(acc[k][:], w12[layer - 1][:, t, :],
                                                z[:, slot12(0, layer, k, i) % RING, j, :],
                                                start=(t == 0), stop=(t == PAIR_TILES - 1))
                    last.then_inc(z_used, 1)

            def mlp1(g):
                pe.wait_ge(r01_summed, g + 1)
                pe.wait_ge(r2_summed, g + 1)
                for t in range(T1):
                    m = slice(t * P, (t + 1) * P)
                    nc.tensor.matmul(h1_ps[:, t, :], wt1[:, 0, m], zs01[:], start=True, stop=False)
                    nc.tensor.matmul(h1_ps[:, t, :], wt1[:, 1, m], zs2[:], start=False, stop=False)
                    last = nc.tensor.matmul(h1_ps[:, t, :], wt1d[:, m], dense[:, bass.ds(g * P, P)],
                                            start=False, stop=True)
                last.then_inc(mlp1_done, 1)

            def mlp2(g):
                pe.wait_ge(h1_ready, g + 1)
                for t in range(T2):
                    for s in range(T1):
                        last = nc.tensor.matmul(h2_ps[:, t, :], wt2[:, s, t * P:(t + 1) * P], h1[:, s, :],
                                                start=(s == 0), stop=(s == T1 - 1))
                last.then_inc(mlp2_done, 1)

            def mlp3(g):
                pe.wait_ge(h2_ready, g + 1)
                for s in range(T2):
                    last = nc.tensor.matmul(h2_ps[0:1, 2, :], wt3[:, s:s + 1], h2[:, s, :],
                                            start=(s == 0), stop=(s == T2 - 1))
                last.then_inc(mlp3_done, 1)

            pe.wait_ge(pad_zeroed, 1)
            pe.wait_ge(ident_made, 1)
            transposes(0, first=True)
            pe.wait_ge(w0_folded, 1)
            for k in range(K):
                layer0(0, k, first=True)
            for n in range(2):
                pe.wait_ge(w_loaded[n], 16)
            pe.wait_ge(small_loaded, 16 * len(SMALL))
            with pe.Fori(0, GROUPS - 1) as g:
                for k in range(K):
                    layer12(g, 1, k)
                transposes(g + 1)
                for k in range(K):
                    layer12(g, 2, k)
                for k in range(K):
                    layer0(g + 1, k)
                    if k == 2:
                        mlp1(g)
                mlp2(g)
                mlp3(g)
            for layer in (1, 2):
                for k in range(K):
                    layer12(GROUPS - 1, layer, k)
            mlp1(GROUPS - 1)
            mlp2(GROUPS - 1)
            mlp3(GROUPS - 1)

        @block.scalar
        def _(act):
            def copy_xt(g, first=False):
                if not first:
                    act.wait_ge(x_stored, 32 * g)
                for k in range(K):
                    act.wait_ge(x_transposed, K * g + k + 1)
                    nc.scalar.copy(xt[:, k, :], xt_ps[k % 2][0:FP, :]).then_inc(xt_copied, 1)
                act.wait_ge(xt_copied, K * (g + 1))
                for copy in range(2):
                    act.dma_start(x_rows[g, :, FP * copy:FP * (copy + 1)].rearrange("k f n -> f k n"),
                                  xt[:]).then_inc(x_stored, 16)

            def relu(out, in_, col):
                rows = slice(out.start_partition(), out.start_partition() + out.shape[0])
                return nc.scalar.activation(out, in_, ACT.Relu, bias=bias[rows, col:col + 1])

            def hidden(g, layer, k, rows):
                relu(hst[rows, k, :], acc[k][rows, :], layer).then_inc(h_copied, 1)

            def store_hidden(g, layer, k, rows):
                act.wait_ge(h_copied, 2 * K * g + K * layer + k + 1)
                act.dma_start(h_rows[layer][g, k], hst[rows, k, :]).then_inc(h_stored[layer][k], 16)

            low, high = slice(0, H), slice(H, S)

            def layer0(g, k, first=False):
                act.wait_ge(z_used, slot0(g, k, 1) + 1)
                hidden(g, 0, k, low)
                store_hidden(g, 0, k, low)
                if not first:
                    act.wait_ge(r01_summed, g)
                relu(r01[high, k, :], acc[k][high, :], 0).then_inc(acc_copied, 1)

            def layer1(g, k):
                act.wait_ge(z_used, slot12(g, 1, k, QI - 1) + 1)
                hidden(g, 1, k, high)
                store_hidden(g, 1, k, high)
                relu(r01[low, k, :], acc[k][low, :], 1).then_inc(acc_copied, 1)

            def layer2(g, k):
                act.wait_ge(z_used, slot12(g, 2, k, QI - 1) + 1)
                relu(r2[:, k, :], acc[k][:], 2).then_inc(acc_copied, 1)

            def mlp1(g):
                act.wait_ge(mlp1_done, g + 1)
                for t in range(T1):
                    last = nc.scalar.activation(h1[:, t, :], h1_ps[:, t, :], ACT.Relu, bias=bt1[:, t:t + 1])
                last.then_inc(h1_ready, 1)

            def mlp2(g):
                act.wait_ge(mlp2_done, g + 1)
                for t in range(T2):
                    last = nc.scalar.activation(h2[:, t, :], h2_ps[:, t, :], ACT.Relu, bias=bt2[:, t:t + 1])
                last.then_inc(h2_ready, 1)

            def mlp3(g):
                act.wait_ge(mlp3_done, g + 1)
                nc.scalar.copy(y[:, bass.ds(g * P, P)], h2_ps[0:1, 2, :]).then_inc(y_ready, 1)

            act.wait_ge(small_loaded, 16 * len(SMALL))
            copy_xt(0, first=True)
            for k in range(K):
                layer0(0, k, first=True)
            with act.Fori(0, GROUPS - 1) as g:
                for k in range(K):
                    layer1(g, k)
                copy_xt(g + 1)
                for k in range(K):
                    layer2(g, k)
                for k in range(K):
                    layer0(g + 1, k)
                    if k == 2:
                        mlp1(g)
                mlp2(g)
                mlp3(g)
            for k in range(K):
                layer1(GROUPS - 1, k)
            for k in range(K):
                layer2(GROUPS - 1, k)
            mlp1(GROUPS - 1)
            mlp2(GROUPS - 1)
            mlp3(GROUPS - 1)
            act.wait_ge(y_ready, GROUPS)
            act.dma_start(io["out"], y[:]).then_inc(y_stored, 16)
            act.wait_ge(y_stored, 16)


def tile_rows0(W):
    Wp = np.zeros((FP, FP, S), W.dtype)
    Wp[:FIELDS, :FIELDS] = W.reshape(FIELDS, FIELDS, S)
    ab, ba = np.zeros((2, ROWS0, sum(TILES0), S), W.dtype)
    t = 0
    for u, tiles in enumerate(TILES0):
        for v in range(4 - tiles, 4):
            for c in range(ROT):
                for f in range(FP):
                    a, b = (f + FAR * u) % FP, (f + ROT * v + c) % FP
                    ab[FP * c + f, t] = Wp[a, b]
                    if (a - b) % FP not in (0, FP // 2):
                        ba[FP * c + f, t] = Wp[b, a]
            t += 1
    return ab, ba


def tile_rows12(W, maps):
    Wp = np.zeros((QN * QI, H, S), W.dtype)
    Wp[:FIELDS] = W.reshape(FIELDS, H, S)[:, :, maps]
    return Wp.reshape(QN, QI, RN, RJ, S).transpose(2, 0, 1, 3, 4).reshape(P, PAIR_TILES, S)


def kernel(**inputs):
    import concourse.bacc as bacc
    from concourse.bass_utils import run_bass_kernel_spmd

    a = {name: np.asarray(v) for name, v in inputs.items()}
    direct_first = np.r_[H:S, 0:H]
    w0a, w0b = tile_rows0(a["L0_rec_W0"])
    top1 = a["W_top1"]
    arrays = {
        "ids": a["ids"].reshape(GROUPS, P, FIELDS),
        "w0a": w0a, "w0b": w0b,
        "w1": tile_rows12(a["L0_rec_W1"], direct_first),
        "w2": tile_rows12(a["L0_rec_W2"], np.arange(S)),
        "wt1": np.stack([np.concatenate([top1[H:S], top1[0:H]]), top1[S:2 * S]], axis=1),
        "wt1d": top1[2 * S:],
        "wt2": a["W_top2"].reshape(T1, P, M2).transpose(1, 0, 2),
        "wt3": a["W_top3"].reshape(T2, P).T,
        "bias": np.stack([a["L0_rec_b0"], a["L0_rec_b1"][direct_first], a["L0_rec_b2"]], axis=1),
        "bt1": a["b_top1"].reshape(T1, P).T,
        "bt2": a["b_top2"].reshape(T2, P).T,
        "dense": a["dense_ctx"].T,
    }
    arrays |= {f"tbl_{f}": a[f"tbl_{f}"] for f in range(FIELDS)}
    arrays = {name: np.ascontiguousarray(v) for name, v in arrays.items()}

    nc = bacc.Bacc("TRN2", target_bir_lowering=False, num_devices=1)
    io = {name: nc.dram_tensor("in_" + name, v.shape, mybir.dt.from_np(v.dtype), kind="ExternalInput").ap()
          for name, v in arrays.items()}
    io["out"] = nc.dram_tensor("out_y", (1, BATCH), F32, kind="ExternalOutput").ap()
    build(nc, io, [io[f"tbl_{f}"] for f in range(FIELDS)])
    r = run_bass_kernel_spmd(nc, [{"in_" + name: v for name, v in arrays.items()}], core_ids=[0])
    return r.results[0]["out_y"].reshape(BATCH, 1)
```

```python
from contextlib import ExitStack

import numpy as np
import concourse.bass as bass
from concourse import mybir

F32 = mybir.dt.float32
F32R = mybir.dt.float32r
I32 = mybir.dt.int32
U32 = mybir.dt.uint32
ALU = mybir.AluOpType
ACT = mybir.ActivationFunctionType
AX = mybir.AxisListType

P = 128
FIELDS = 39
FP = 40
D = 16
XGF = 72
BATCH = 1024
GROUPS = BATCH // P
K = 4
CHUNKS = GROUPS * K
DK = D // K
N = DK * P
S = 128
H = 64
QI, QN = 5, 8
RJ, RN = 4, 16
PAIR_TILES = QI * RJ
ROT, ROWS0 = 3, 3 * FP
FAR = 23
TILES0 = (4, 3)
DOUBLE = 2 * FP
M1, M2 = 512, 256
T1, T2 = M1 // P, M2 // P
DENSE = 16

SPLIT_OPS = ((0,), (0, 1), (0, 1))
PLAIN_OPS = ((1,), (2, 3, 4), (2, 3, 4))
ORDER = ((1, 0), (2, 0, 3, 1, 4), (2, 0, 3, 1, 4))
PLAIN_RING, SPLIT_RING, ACC_RING = 4, 2, 4
SPLIT_TILE = (0, 4, 12)
SPLIT_TILES = 20


class Chunk:

    def __init__(self, g, k, first=None):
        self.g, self.k = g, k
        self.c = K * g + k
        self.edge = self.c if isinstance(self.c, int) else None
        self.like = Chunk(first, k) if first is not None else self


def count_before(sizes, layer, chunk):
    a, b, c = sizes
    step = chunk.c + layer - 2
    if chunk.edge is None or 0 <= chunk.edge + layer - 2 <= CHUNKS - 3:
        return 2 * a + b + (a + b + c) * step + (0, a, a + b)[layer]
    if step < 0:
        return (step + 2) * a + (0, a, 0)[layer]
    full = 2 * a + b + (a + b + c) * (CHUNKS - 2)
    return full + (step - (CHUNKS - 2)) * (b + c) + (0, 0, b if step == CHUNKS - 2 else 0)[layer]


def plain_no(layer, chunk, op):
    return count_before([len(x) for x in PLAIN_OPS], layer, chunk) + PLAIN_OPS[layer].index(op)


def split_no(layer, chunk, op):
    return count_before([len(x) for x in SPLIT_OPS], layer, chunk) + SPLIT_OPS[layer].index(op)


def acc_no(layer, chunk):
    return count_before([1, 1, 1], layer, chunk)


def build(nc, io, tables):
    ctx = ExitStack()
    with ctx:
        def sb(name, shape, dt=F32):
            return ctx.enter_context(nc.sbuf_tensor(name, shape, dt))

        def ps(name, shape):
            return ctx.enter_context(nc.psum_tensor(name, shape, F32))

        def sem(name):
            return ctx.enter_context(nc.semaphore(name))

        x_rows = nc.dram_tensor("x_rows", (GROUPS, K, DOUBLE, N), F32).ap()
        h_rows = [nc.dram_tensor(f"h{n}_rows", (GROUPS, K, H, N), F32).ap() for n in (1, 2)]

        wp0 = sb("wp0", [ROWS0, TILES0[1], S])
        wp12 = [sb(f"wp{n}", [P, RJ * len(PLAIN_OPS[n]), S]) for n in (1, 2)]
        ws = sb("ws", [P, 2, SPLIT_TILES, S], F32R)
        wt1 = sb("wt1", [P, 2, M1])
        wt1d = sb("wt1d", [DENSE, M1])
        wt2 = sb("wt2", [P, T1, M2])
        wt3 = sb("wt3", [P, T2])
        bias = sb("bias", [P, 3])
        bt1 = sb("bt1", [P, T1])
        bt2 = sb("bt2", [P, T2])
        dense_y = sb("dense_y", [33, BATCH])
        dense = dense_y[0:DENSE, :]
        y = dense_y[32:33, :]
        ident = sb("ident", [P, P])
        ids = sb("ids", [P, FIELDS], I32)
        xg = sb("xg", [P, XGF, D])
        xt = sb("xt", [FP, 2, N])
        lx = sb("lx", [ROWS0, 2, N])
        ly = sb("ly", [ROWS0, 4, N])
        xa = sb("xa", [P, 2, QI, N])
        hb = [sb(f"hb{n}", [P, RJ, N]) for n in (1, 2)]
        zp = sb("zp", [P, PLAIN_RING, 4, N])
        zs = sb("zs", [P, SPLIT_RING, 4, N])
        zh = sb("zh", [P, SPLIT_RING, 4, N], F32R)
        zl = sb("zl", [P, SPLIT_RING, 4, N], F32R)
        hst = sb("hst", [P, N])
        r01 = sb("r01", [P, K, N])
        r2 = sb("r2", [P, K, N])
        sum01 = sb("sum01", [P, 2, P])
        sum2 = sb("sum2", [P, P])
        h1 = sb("h1", [P, T1, P])
        h2 = sb("h2", [P, T2, P])

        acc = [ps(f"acc{k}", [P, N]) for k in range(ACC_RING)]
        xt_ps = [ps(f"xt_ps{i}", [P, N]) for i in range(2)]
        h1_ps = ps("h1_ps", [P, T1, P])
        h2_ps = ps("h2_ps", [P, 4, P])

        w_loaded = sem("w_loaded")
        wp_loaded = sem("wp_loaded")
        small_loaded = sem("small_loaded")
        w0_folded = sem("w0_folded")
        w_high = sem("w_high")
        w_low = sem("w_low")
        ident_zeroed = sem("ident_zeroed")
        pad_zeroed = sem("pad_zeroed")
        ident_made = sem("ident_made")
        ids_loaded = sem("ids_loaded")
        gathered = sem("gathered")
        x_transposed = sem("x_transposed")
        xt_copied = sem("xt_copied")
        x_stored = [sem(f"x_stored{i}") for i in range(2)]
        l0_loaded = sem("l0_loaded")
        xa_loaded = [sem(f"xa_loaded{i}") for i in range(2)]
        hb_loaded = [sem(f"hb{n}_loaded") for n in (1, 2)]
        plain_ready = sem("plain_ready")
        plain_used = sem("plain_used")
        split_product = sem("split_product")
        high_ready = sem("high_ready")
        split_ready = sem("split_ready")
        split_used = sem("split_used")
        acc_copied = sem("acc_copied")
        h_copied = sem("h_copied")
        h_stored = [sem(f"h{n}_stored") for n in (1, 2)]
        r01_halved = sem("r01_halved")
        r01_summed = sem("r01_summed")
        r2_summed = sem("r2_summed")
        mlp1_done = sem("mlp1_done")
        h1_ready = sem("h1_ready")
        mlp2_done = sem("mlp2_done")
        h2_ready = sem("h2_ready")
        mlp3_done = sem("mlp3_done")
        y_ready = sem("y_ready")
        y_stored = sem("y_stored")

        block = ctx.enter_context(nc.Block())

        def steps_of(g, j, first=None):
            f = 0 if first is None else first
            return [Chunk(g + (j + ahead) // K, (j + ahead) % K, None if first is None else f + (j + ahead) // K)
                    for ahead in (2, 1, 0)]

        def edge_step(c):
            return [Chunk(x // K, x % K) if 0 <= x < CHUNKS else None for x in (c + 2, c + 1, c)]

        LAST = CHUNKS - 1
        AFTER_LOOP = range(K * (GROUPS - 1) + 1, CHUNKS)

        def window(view, steps):
            return bass.AP(view.tensor, view.offset, steps)

        SMALL = [(wt1, "wt1"), (wt1d, "wt1d"), (wt2, "wt2"), (wt3, "wt3"), (bias, "bias"), (bt1, "bt1"),
                 (bt2, "bt2"), (dense, "dense")]

        def flat(ap):
            return ap.rearrange("p a s -> p (a s)")

        raw = [zp[0:ROWS0, 2, 0, 0:4 * S], flat(zp[:, 0])[:, 0:8 * S], flat(zp[:, 1])[:, 0:8 * S]]
        w0b = flat(zp[0:ROWS0, 3])[:, 0:7 * S]

        @block.sync
        def _(sp):
            sp.dma_start(raw[0], flat(io["w0a"][:, 0:4])).then_inc(w_loaded, 16)
            sp.dma_start(flat(wp0[:]), flat(io["w0a"][:, 4:7])).then_inc(w_loaded, 16)
            sp.dma_start(w0b, flat(io["w0b"])).then_inc(w_loaded, 16)
            for n in (1, 2):
                sp.dma_start(raw[n], flat(io[f"w{n}"][:, 0:8])).then_inc(w_loaded, 16)
                sp.dma_start(wp12[n - 1][:], io[f"w{n}"][:, 8:]).then_inc(wp_loaded, 16)
            for dst, name in SMALL:
                sp.dma_start(dst[:] if dst is not dense else dst, io[name]).then_inc(small_loaded, 16)

            def load_l0(x):
                sp.wait_ge(x_stored[x.k % 2], 32 * (2 * x.g + x.k // 2 + 1))
                for c in range(ROT):
                    sp.dma_start(lx[FP * c:FP * (c + 1)],
                                 window(x_rows[x.g, x.k], [[N, FP], [FAR * N, 2], [1, N]])).then_inc(l0_loaded, 16)
                    sp.dma_start(ly[FP * c:FP * (c + 1)],
                                 window(x_rows[x.g, x.k, c:c + 1], [[N, FP], [ROT * N, 4], [1, N]])
                                 ).then_inc(l0_loaded, 16)

            def load_xa(x, i):
                sp.dma_start(xa[:, x.k % 2, i], window(x_rows[x.g, x.k, i:i + 1], [[0, RN], [QI * N, QN], [1, N]])
                             ).then_inc(xa_loaded[x.k % 2], 16)

            def load_hb(layer, x):
                sp.wait_ge(h_stored[layer - 1], 16 * (x.c + 1))
                sp.dma_start(hb[layer - 1][:], window(h_rows[layer - 1][x.g, x.k],
                                                      [[RJ * N, RN], [0, QN], [1, RJ * N]])
                             ).then_inc(hb_loaded[layer - 1], 16)

            def used(layer, x, op):
                sp.wait_ge(plain_ready, plain_no(layer, x, op) + 1)

            def step(now, after):
                x0, x1, x2 = now
                n0, n1, n2 = after
                if n0:
                    used(0, x0, 1)
                    load_l0(n0)
                if n1:
                    used(1, x1, QI - 1)
                    load_hb(1, n1)
                    for op, free in ((2, (0, 2)), (3, (1, 3)), (4, (4,))):
                        if x2:
                            used(2, x2, op)
                        for i in free:
                            load_xa(n1, i)
                if n2:
                    if x2:
                        used(2, x2, QI - 1)
                    load_hb(2, n2)

            c0, c1 = Chunk(0, 0), Chunk(0, 1)
            load_l0(c0)
            for i in range(QI):
                load_xa(c0, i)
            used(0, c0, 1)
            load_l0(c1)
            load_hb(1, c0)
            step(edge_step(-1), edge_step(0))
            step(edge_step(0), edge_step(1))
            with sp.Fori(0, GROUPS - 1) as g:
                for j in range(1, K + 1):
                    step(steps_of(g, j, 0), steps_of(g, j + 1, 0))
            for c in AFTER_LOOP:
                step(edge_step(c), edge_step(c + 1))

        @block.gpsimd
        def _(pool):
            def load_ids(g):
                pool.dma_start(ids[:], io["ids"][g]).then_inc(ids_loaded, 16)

            def gather():
                for f in range(FIELDS):
                    nc.gpsimd.indirect_dma_start(
                        xg[:, f, :], None, tables[f],
                        bass.IndirectOffsetOnAxis(ids[:, f:f + 1].bitcast(U32), 0)).then_inc(gathered, 16)

            load_ids(0)
            nc.gpsimd.memset(ident[:], 0.0).then_inc(ident_zeroed, 1)
            nc.gpsimd.memset(xg[:, FIELDS:, :], 0.0).then_inc(pad_zeroed, 1)
            pool.wait_ge(ident_zeroed, 1)
            nc.gpsimd.affine_select(out=ident[:], in_=ident[:], compare_op=ALU.not_equal, fill=1.0, base=0,
                                    pattern=[[-1, P]], channel_multiplier=1).then_inc(ident_made, 1)
            pool.wait_ge(ids_loaded, 16)
            with pool.Fori(0, GROUPS - 1) as g:
                gather()
                pool.wait_ge(gathered, 16 * FIELDS * (g + 1))
                load_ids(g + 1)
                pool.wait_ge(x_transposed, K * (g + 1))
                pool.wait_ge(ids_loaded, 16 * (g + 2))
            gather()

        @block.vector
        def _(dve):
            dve.wait_ge(w_loaded, 16 * 5)
            nc.vector.tensor_tensor(raw[0], raw[0], w0b[:, 0:4 * S], ALU.add).then_inc(w0_folded, 1)
            nc.vector.tensor_tensor(flat(wp0[:]), flat(wp0[:]), w0b[:, 4 * S:], ALU.add).then_inc(w0_folded, 1)
            for layer in range(3):
                rows = ROWS0 if layer == 0 else P
                tiles = slice(SPLIT_TILE[layer], SPLIT_TILE[layer] + (4 if layer == 0 else 8))
                dve.wait_ge(w_high, layer + 1)
                nc.vector.tensor_tensor(flat(ws[0:rows, 1, tiles]), raw[layer],
                                        flat(ws[0:rows, 0, tiles]).bitcast(F32), ALU.subtract).then_inc(w_low, 1)

            dve.wait_ge(w_low, 3)

            def operands(layer, x, op):
                if layer == 0:
                    tiles = TILES0[op]
                    return (lx[:, op:op + 1, :].to_broadcast([ROWS0, tiles, N]), ly[:, 4 - tiles:4, :])
                return xa[:, x.k % 2, op:op + 1, :].to_broadcast([P, RJ, N]), hb[layer - 1][:]

            def z_slot(ring, n, layer, tiles=4):
                return ring[0:ROWS0 if layer == 0 else P, n, 0:tiles, :]

            def plain(layer, x, op):
                n = plain_no(layer, x, op)
                if x.edge is None or n >= PLAIN_RING:
                    dve.wait_ge(plain_used, n - PLAIN_RING + 1)
                a, b = operands(layer, x, op)
                out = z_slot(zp, plain_no(layer, x.like, op) % PLAIN_RING, layer, TILES0[1] if layer == 0 else 4)
                nc.vector.tensor_tensor(out, a, b, ALU.mult).then_inc(plain_ready, 1)

            def split(layer, x, op):
                n = split_no(layer, x, op)
                if x.edge is None or n >= SPLIT_RING:
                    dve.wait_ge(split_ready, n - SPLIT_RING + 1)
                a, b = operands(layer, x, op)
                out = z_slot(zs, split_no(layer, x.like, op) % SPLIT_RING, layer)
                nc.vector.tensor_tensor(out, a, b, ALU.mult).then_inc(split_product, 1)

            def low(layer, x, op):
                n = split_no(layer, x.like, op) % SPLIT_RING
                dve.wait_ge(high_ready, split_no(layer, x, op) + 1)
                nc.vector.tensor_tensor(z_slot(zl, n, layer), z_slot(zs, n, layer),
                                        z_slot(zh, n, layer).bitcast(F32), ALU.subtract).then_inc(split_ready, 1)

            def sum_positions(out, r, done):
                nc.vector.tensor_reduce(out, r.rearrange("p k (d b) -> p b (k d)", b=P), AX.X,
                                        ALU.add).then_inc(done, 1)

            def half01(x):
                half = x.k // 2
                dve.wait_ge(acc_copied, acc_no(1, x) + 1)
                sum_positions(sum01[:, half, :], r01[:, x.k - 1:x.k + 1], r01_halved)
                if half:
                    dve.wait_ge(r01_halved, 2 * (x.g + 1))
                    nc.vector.tensor_tensor(sum01[:, 1, :], sum01[:, 0, :], sum01[:, 1, :],
                                            ALU.add).then_inc(r01_summed, 1)

            def all2(x):
                dve.wait_ge(acc_copied, acc_no(2, x) + 1)
                sum_positions(sum2[:], r2[:], r2_summed)

            def step(now, odd=False, group_done=None):
                x0, x1, x2 = now
                if x0:
                    dve.wait_ge(l0_loaded, 16 * 2 * ROT * (x0.c + 1))
                    split(0, x0, 0)
                    plain(0, x0, 1)
                if x1:
                    dve.wait_ge(xa_loaded[x1.k % 2], 16 * QI * (2 * x1.g + x1.k // 2 + 1))
                    dve.wait_ge(hb_loaded[0], 16 * (x1.c + 1))
                    split(1, x1, 0)
                if x0:
                    low(0, x0, 0)
                if odd:
                    half01(x2)
                if x1:
                    plain(1, x1, 2)
                    split(1, x1, 1)
                    low(1, x1, 0)
                    plain(1, x1, 3)
                    low(1, x1, 1)
                    if group_done:
                        all2(group_done)
                    plain(1, x1, 4)
                if x2:
                    dve.wait_ge(hb_loaded[1], 16 * (x2.c + 1))
                    split(2, x2, 0)
                    plain(2, x2, 2)
                    split(2, x2, 1)
                    low(2, x2, 0)
                    plain(2, x2, 3)
                    low(2, x2, 1)
                    plain(2, x2, 4)

            for c in (-2, -1, 0):
                step(edge_step(c))
            with dve.Fori(0, GROUPS - 1) as g:
                for j in range(1, K + 1):
                    step(steps_of(g, j, 0), odd=j % 2 == 1, group_done=Chunk(g, K - 1, 0) if j == K else None)
            for c in AFTER_LOOP:
                step(edge_step(c), odd=c % 2 == 1)
            all2(Chunk(GROUPS - 1, K - 1))

        @block.tensor
        def _(pe):
            def transpose(g, k):
                pe.wait_ge(gathered, 16 * FIELDS * (g + 1))
                if k >= 2 or not isinstance(g, int):
                    pe.wait_ge(xt_copied, K * g + k - 1)
                for d in range(DK):
                    last = nc.tensor.transpose(xt_ps[k % 2][0:XGF, d * P:(d + 1) * P], xg[:, :, k * DK + d],
                                               ident[:])
                last.then_inc(x_transposed, 1)

            def layer_ops(layer, x, ops):
                rows = ROWS0 if layer == 0 else P
                a = acc_no(layer, x)
                out = acc[acc_no(layer, x.like) % ACC_RING][:]
                for op in ops:
                    first, final = op == ORDER[layer][0], op == ORDER[layer][-1]
                    if first and (x.edge is None or a >= ACC_RING):
                        pe.wait_ge(acc_copied, a - ACC_RING + 1)
                    tiles = TILES0[op] if layer == 0 else RJ
                    if op in PLAIN_OPS[layer]:
                        pe.wait_ge(plain_ready, plain_no(layer, x, op) + 1)
                        slot = plain_no(layer, x.like, op) % PLAIN_RING
                        w = wp0 if layer == 0 else wp12[layer - 1]
                        t0 = 0 if layer == 0 else RJ * (op - 2)
                        passes = [(w[:, t0 + j, :], zp[0:rows, slot, j, :]) for j in range(tiles)]
                        used = plain_used
                    else:
                        pe.wait_ge(split_ready, split_no(layer, x, op) + 1)
                        slot = split_no(layer, x.like, op) % SPLIT_RING
                        t0 = SPLIT_TILE[layer] + RJ * op
                        passes = []
                        for j in range(tiles):
                            high, low = ws[0:rows, 0, t0 + j, :], ws[0:rows, 1, t0 + j, :]
                            zhj, zlj = zh[0:rows, slot, j, :], zl[0:rows, slot, j, :]
                            passes += [(low, zhj), (high, zlj), (high, zhj)]
                        used = split_used
                    for n, (w, z) in enumerate(passes):
                        last = nc.tensor.matmul(out, w, z, start=(first and n == 0),
                                                stop=(final and n == len(passes) - 1))
                    last.then_inc(used, 1)

            def mlp1(g):
                pe.wait_ge(r01_summed, g + 1)
                pe.wait_ge(r2_summed, g + 1)
                for t in range(T1):
                    m = slice(t * P, (t + 1) * P)
                    nc.tensor.matmul(h1_ps[:, t, :], wt1[:, 0, m], sum01[:, 1, :], start=True, stop=False)
                    nc.tensor.matmul(h1_ps[:, t, :], wt1[:, 1, m], sum2[:], start=False, stop=False)
                    last = nc.tensor.matmul(h1_ps[:, t, :], wt1d[:, m], dense[:, bass.ds(g * P, P)],
                                            start=False, stop=True)
                last.then_inc(mlp1_done, 1)

            def mlp2(g):
                pe.wait_ge(h1_ready, g + 1)
                for t in range(T2):
                    for s in range(T1):
                        last = nc.tensor.matmul(h2_ps[:, t, :], wt2[:, s, t * P:(t + 1) * P], h1[:, s, :],
                                                start=(s == 0), stop=(s == T1 - 1))
                last.then_inc(mlp2_done, 1)

            def mlp3(g):
                pe.wait_ge(h2_ready, g + 1)
                for s in range(T2):
                    last = nc.tensor.matmul(h2_ps[0:1, 2, :], wt3[:, s:s + 1], h2[:, s, :],
                                            start=(s == 0), stop=(s == T2 - 1))
                last.then_inc(mlp3_done, 1)

            def step(now, j=0, next_group=None, group_done=None):
                x0, x1, x2 = now
                if next_group is not None and j <= 2:
                    transpose(next_group, 0 if j == 1 else 3)
                if x0:
                    layer_ops(0, x0, ORDER[0])
                if next_group is not None and j == 1:
                    transpose(next_group, 1)
                if x1:
                    layer_ops(1, x1, ORDER[1])
                if next_group is not None and j == 1:
                    transpose(next_group, 2)
                if group_done is not None:
                    mlp1(group_done)
                if x2:
                    layer_ops(2, x2, ORDER[2][:2])
                    if group_done is not None:
                        mlp2(group_done)
                    layer_ops(2, x2, ORDER[2][2:3])
                    if group_done is not None:
                        mlp3(group_done)
                    layer_ops(2, x2, ORDER[2][3:])

            pe.wait_ge(pad_zeroed, 1)
            pe.wait_ge(ident_made, 1)
            for k in range(K):
                transpose(0, k)
            pe.wait_ge(w0_folded, 2)
            pe.wait_ge(w_low, 3)
            pe.wait_ge(wp_loaded, 32)
            pe.wait_ge(small_loaded, 16 * len(SMALL))
            for c in (-2, -1, 0):
                step(edge_step(c))
            with pe.Fori(0, GROUPS - 1) as g:
                for j in range(1, K + 1):
                    step(steps_of(g, j, 0), j, next_group=g + 1 if j <= 2 else None,
                         group_done=g if j == K else None)
            for c in AFTER_LOOP:
                step(edge_step(c))
            mlp1(GROUPS - 1)
            mlp2(GROUPS - 1)
            mlp3(GROUPS - 1)

        @block.scalar
        def _(act):
            def high(layer, x, op):
                n = split_no(layer, x, op)
                slot = split_no(layer, x.like, op) % SPLIT_RING
                rows = ROWS0 if layer == 0 else P
                if x.edge is None or n >= SPLIT_RING:
                    act.wait_ge(split_used, n - SPLIT_RING + 1)
                act.wait_ge(split_product, n + 1)
                nc.scalar.copy(zh[0:rows, slot], zs[0:rows, slot]).then_inc(high_ready, 1)

            def copy_xt(g, k):
                if k >= 2 or not isinstance(g, int):
                    act.wait_ge(x_stored[k % 2], 32 * (2 * g + k // 2))
                act.wait_ge(x_transposed, K * g + k + 1)
                nc.scalar.copy(xt[:, k % 2, :], xt_ps[k % 2][0:FP, :]).then_inc(xt_copied, 1)
                act.wait_ge(xt_copied, K * g + k + 1)
                for copy in range(2):
                    act.dma_start(x_rows[g, k, FP * copy:FP * (copy + 1)], xt[:, k % 2, :]
                                  ).then_inc(x_stored[k % 2], 16)

            def relu(out, in_, col):
                rows = slice(out.start_partition(), out.start_partition() + out.shape[0])
                return nc.scalar.activation(out, in_, ACT.Relu, bias=bias[rows, col:col + 1])

            def hidden(layer, x, src, rows):
                n = count_before([1, 1, 0], layer, x)
                relu(hst[rows, :], src[rows, :], layer).then_inc(h_copied, 1)
                act.wait_ge(h_copied, n + 1)
                act.dma_start(h_rows[layer][x.g, x.k], hst[rows, :]).then_inc(h_stored[layer], 16)

            low_rows, high_rows = slice(0, H), slice(H, S)

            def out0(x):
                act.wait_ge(split_used, split_no(0, x, 0) + 1)
                src = acc[acc_no(0, x.like) % ACC_RING]
                if x.edge == 1:
                    act.wait_ge(h_stored[0], 16)
                hidden(0, x, src, low_rows)
                if x.k % 2 == 0 and (x.edge is None or x.edge >= K):
                    act.wait_ge(r01_halved, 2 * x.g + x.k // 2 - 1)
                relu(r01[high_rows, x.k, :], src[high_rows, :], 0).then_inc(acc_copied, 1)

            def out1(x):
                act.wait_ge(plain_used, plain_no(1, x, QI - 1) + 1)
                src = acc[acc_no(1, x.like) % ACC_RING]
                hidden(1, x, src, high_rows)
                relu(r01[low_rows, x.k, :], src[low_rows, :], 1).then_inc(acc_copied, 1)

            def out2(x):
                act.wait_ge(plain_used, plain_no(2, x, QI - 1) + 1)
                relu(r2[:, x.k, :], acc[acc_no(2, x.like) % ACC_RING][:], 2).then_inc(acc_copied, 1)

            def mlp1(g):
                act.wait_ge(mlp1_done, g + 1)
                for t in range(T1):
                    last = nc.scalar.activation(h1[:, t, :], h1_ps[:, t, :], ACT.Relu, bias=bt1[:, t:t + 1])
                last.then_inc(h1_ready, 1)

            def mlp2(g):
                act.wait_ge(mlp2_done, g + 1)
                for t in range(T2):
                    last = nc.scalar.activation(h2[:, t, :], h2_ps[:, t, :], ACT.Relu, bias=bt2[:, t:t + 1])
                last.then_inc(h2_ready, 1)

            def mlp3(g):
                act.wait_ge(mlp3_done, g + 1)
                nc.scalar.copy(y[:, bass.ds(g * P, P)], h2_ps[0:1, 2, :]).then_inc(y_ready, 1)

            def step(now, before2=None, j=0, next_group=None, group_done=None):
                x0, x1, x2 = now
                if x0:
                    high(0, x0, 0)
                if next_group is not None and j <= 2:
                    copy_xt(next_group, 0 if j == 1 else 3)
                if x1:
                    high(1, x1, 0)
                if before2:
                    out2(before2)
                if x1:
                    high(1, x1, 1)
                if x0:
                    out0(x0)
                if next_group is not None and j == 1:
                    copy_xt(next_group, 1)
                if x2:
                    high(2, x2, 0)
                    high(2, x2, 1)
                if x1:
                    out1(x1)
                if next_group is not None and j == 1:
                    copy_xt(next_group, 2)
                if group_done is not None:
                    mlp1(group_done)
                    mlp2(group_done)
                    mlp3(group_done)

            act.wait_ge(w_loaded, 16 * 5)
            act.wait_ge(w0_folded, 1)
            for layer in range(3):
                rows = ROWS0 if layer == 0 else P
                tiles = slice(SPLIT_TILE[layer], SPLIT_TILE[layer] + (4 if layer == 0 else 8))
                nc.scalar.copy(flat(ws[0:rows, 0, tiles]), raw[layer]).then_inc(w_high, 1)
            act.wait_ge(small_loaded, 16 * len(SMALL))
            for k in range(K):
                copy_xt(0, k)
            for c in (-2, -1, 0):
                step(edge_step(c))
            with act.Fori(0, GROUPS - 1) as g:
                for j in range(1, K + 1):
                    step(steps_of(g, j, 0), Chunk(g, j - 1, 0), j, next_group=g + 1 if j <= 2 else None,
                         group_done=g if j == K else None)
            for c in AFTER_LOOP:
                step(edge_step(c), edge_step(c - 1)[2])
            out2(Chunk(GROUPS - 1, K - 1))
            mlp1(GROUPS - 1)
            mlp2(GROUPS - 1)
            mlp3(GROUPS - 1)
            act.wait_ge(y_ready, GROUPS)
            act.dma_start(io["out"], y).then_inc(y_stored, 16)
            act.wait_ge(y_stored, 16)


def tile_rows0(W):
    Wp = np.zeros((FP, FP, S), W.dtype)
    Wp[:FIELDS, :FIELDS] = W.reshape(FIELDS, FIELDS, S)
    ab, ba = np.zeros((2, ROWS0, sum(TILES0), S), W.dtype)
    t = 0
    for u, tiles in enumerate(TILES0):
        for v in range(4 - tiles, 4):
            for c in range(ROT):
                for f in range(FP):
                    a, b = (f + FAR * u) % FP, (f + ROT * v + c) % FP
                    ab[FP * c + f, t] = Wp[a, b]
                    if (a - b) % FP not in (0, FP // 2):
                        ba[FP * c + f, t] = Wp[b, a]
            t += 1
    return ab, ba


def tile_rows12(W, maps):
    Wp = np.zeros((QN * QI, H, S), W.dtype)
    Wp[:FIELDS] = W.reshape(FIELDS, H, S)[:, :, maps]
    return Wp.reshape(QN, QI, RN, RJ, S).transpose(2, 0, 1, 3, 4).reshape(P, PAIR_TILES, S)


def kernel(**inputs):
    import concourse.bacc as bacc
    from concourse.bass_utils import run_bass_kernel_spmd

    a = {name: np.asarray(v) for name, v in inputs.items()}
    direct_first = np.r_[H:S, 0:H]
    w0a, w0b = tile_rows0(a["L0_rec_W0"])
    top1 = a["W_top1"]
    arrays = {
        "ids": a["ids"].reshape(GROUPS, P, FIELDS),
        "w0a": w0a, "w0b": w0b,
        "w1": tile_rows12(a["L0_rec_W1"], direct_first),
        "w2": tile_rows12(a["L0_rec_W2"], np.arange(S)),
        "wt1": np.stack([np.concatenate([top1[H:S], top1[0:H]]), top1[S:2 * S]], axis=1),
        "wt1d": top1[2 * S:],
        "wt2": a["W_top2"].reshape(T1, P, M2).transpose(1, 0, 2),
        "wt3": a["W_top3"].reshape(T2, P).T,
        "bias": np.stack([a["L0_rec_b0"], a["L0_rec_b1"][direct_first], a["L0_rec_b2"]], axis=1),
        "bt1": a["b_top1"].reshape(T1, P).T,
        "bt2": a["b_top2"].reshape(T2, P).T,
        "dense": a["dense_ctx"].T,
    }
    arrays |= {f"tbl_{f}": a[f"tbl_{f}"] for f in range(FIELDS)}
    arrays = {name: np.ascontiguousarray(v) for name, v in arrays.items()}

    nc = bacc.Bacc("TRN2", target_bir_lowering=False, num_devices=1)
    io = {name: nc.dram_tensor("in_" + name, v.shape, mybir.dt.from_np(v.dtype), kind="ExternalInput").ap()
          for name, v in arrays.items()}
    io["out"] = nc.dram_tensor("out_y", (1, BATCH), F32, kind="ExternalOutput").ap()
    build(nc, io, [io[f"tbl_{f}"] for f in range(FIELDS)])
    r = run_bass_kernel_spmd(nc, [{"in_" + name: v for name, v in arrays.items()}], core_ids=[0])
    return r.results[0]["out_y"].reshape(BATCH, 1)
```

```python
from contextlib import ExitStack

import numpy as np
import concourse.bass as bass
from concourse import mybir

F32 = mybir.dt.float32
F32R = mybir.dt.float32r
I32 = mybir.dt.int32
U32 = mybir.dt.uint32
ALU = mybir.AluOpType
ACT = mybir.ActivationFunctionType
AX = mybir.AxisListType

P = 128
FIELDS = 39
FP = 40
D = 16
BATCH = 1024
GROUPS = BATCH // P
K = 4
CHUNKS = GROUPS * K
B = P // K
N = D * B
E = P // B
GATHERS = FP // E
HALF = GATHERS // 2 * D
S = 128
H = 64
QI, QN = 5, 8
RJ, RN = 4, 16
PAIR_TILES = QI * RJ
ROT, ROWS0 = 3, 3 * FP
FAR = 23
TILES0 = (4, 3)
AGAIN = 25
M1, M2 = 512, 256
T1, T2 = M1 // P, M2 // P
DENSE = 16

SPLIT_OPS = ((1,), (0, 1), (0, 1))
PLAIN_OPS = ((0,), (2, 3, 4), (2, 3, 4))
ORDER = ((0, 1), (2, 0, 3, 1, 4), (2, 0, 3, 1, 4))
PLAIN_RING, SPLIT_RING, ACC_RING = 4, 2, 4
SPLIT_COUNT = (TILES0[1], 2 * RJ, 2 * RJ)
SPLIT_TILE = (0, SPLIT_COUNT[0], SPLIT_COUNT[0] + SPLIT_COUNT[1])
SPLIT_TILES = sum(SPLIT_COUNT)


class Chunk:

    def __init__(self, g, k, first=None):
        self.g, self.k = g, k
        self.c = K * g + k
        self.edge = self.c if isinstance(self.c, int) else None
        self.like = Chunk(first, k) if first is not None else self


def count_before(sizes, layer, chunk):
    a, b, c = sizes
    step = chunk.c + layer - 2
    if chunk.edge is None or 0 <= chunk.edge + layer - 2 <= CHUNKS - 3:
        return 2 * a + b + (a + b + c) * step + (0, a, a + b)[layer]
    if step < 0:
        return (step + 2) * a + (0, a, 0)[layer]
    full = 2 * a + b + (a + b + c) * (CHUNKS - 2)
    return full + (step - (CHUNKS - 2)) * (b + c) + (0, 0, b if step == CHUNKS - 2 else 0)[layer]


def plain_no(layer, chunk, op):
    return count_before([len(x) for x in PLAIN_OPS], layer, chunk) + PLAIN_OPS[layer].index(op)


def split_no(layer, chunk, op):
    return count_before([len(x) for x in SPLIT_OPS], layer, chunk) + SPLIT_OPS[layer].index(op)


def acc_no(layer, chunk):
    return count_before([1, 1, 1], layer, chunk)


def build(nc, io):
    ctx = ExitStack()
    with ctx:
        def sb(name, shape, dt=F32):
            return ctx.enter_context(nc.sbuf_tensor(name, shape, dt))

        def ps(name, shape):
            return ctx.enter_context(nc.psum_tensor(name, shape, F32))

        def sem(name):
            return ctx.enter_context(nc.semaphore(name))

        x_rows = nc.dram_tensor("x_rows", (GROUPS, K, FP + AGAIN, N), F32).ap()
        h_rows = [nc.dram_tensor(f"h{n}_rows", (GROUPS, K, H, N), F32).ap() for n in (1, 2)]

        wp0 = sb("wp0", [ROWS0, TILES0[0], S])
        wp12 = [sb(f"wp{n}", [P, RJ * len(PLAIN_OPS[n]), S]) for n in (1, 2)]
        ws = sb("ws", [P, 2, SPLIT_TILES, S], F32R)
        wt1 = sb("wt1", [P, 2, M1])
        wt1d = sb("wt1d", [DENSE, M1])
        wt2 = sb("wt2", [P, T1, M2])
        wt3 = sb("wt3", [P, T2])
        bias = sb("bias", [P, 3])
        bt1 = sb("bt1", [P, T1])
        bt2 = sb("bt2", [P, T2])
        dense_y = sb("dense_y", [33, BATCH])
        dense = dense_y[0:DENSE, :]
        y = dense_y[32:33, :]
        ident = sb("ident", [P, P])
        ids = sb("ids", [P, K, GATHERS], I32)
        table_start = sb("table_start", [P, GATHERS], I32)
        index = sb("index", [P, K, GATHERS], I32)
        xg = sb("xg", [P, K, GATHERS, D])
        xt = sb("xt", [HALF, 2, 2, E, B])
        lx = sb("lx", [ROWS0, 2, N])
        ly = sb("ly", [ROWS0, 4, N])
        xa = sb("xa", [P, 2, QI, N])
        hb = [sb(f"hb{n}", [P, RJ, N]) for n in (1, 2)]
        zp = sb("zp", [P, PLAIN_RING, 4, N])
        zs = sb("zs", [P, SPLIT_RING, 4, N])
        zh = sb("zh", [P, SPLIT_RING, 4, N], F32R)
        zl = sb("zl", [P, SPLIT_RING, 4, N], F32R)
        hst = sb("hst", [P, N])
        r01 = sb("r01", [P, K, N])
        r2 = sb("r2", [P, K, N])
        sum01 = sb("sum01", [P, K, B])
        sum2 = sb("sum2", [P, K, B])
        h1 = sb("h1", [P, T1, P])
        h2 = sb("h2", [P, T2, P])

        acc = [ps(f"acc{k}", [P, N]) for k in range(ACC_RING)]
        xt_ps = [ps(f"xt_ps{i}", [P, 2, P]) for i in range(2)]
        h1_ps = ps("h1_ps", [P, T1, P])
        h2_ps = ps("h2_ps", [P, 4, P])

        w_loaded = [sem(f"w{n}_loaded") for n in range(3)]
        wp_loaded = [sem(f"wp{n}_loaded") for n in (1, 2)]
        bias_loaded = sem("bias_loaded")
        mlp_loaded = sem("mlp_loaded")
        w0_folded = sem("w0_folded")
        w_high = sem("w_high")
        w_low = sem("w_low")
        ident_zeroed = sem("ident_zeroed")
        ident_made = sem("ident_made")
        ids0_loaded = sem("ids0_loaded")
        ids_loaded = sem("ids_loaded")
        starts_loaded = sem("starts_loaded")
        index_ready = sem("index_ready")
        gathered = [sem(f"gathered{k}") for k in range(K)]
        x_transposed = sem("x_transposed")
        xt_copied = sem("xt_copied")
        x_stored = [sem(f"x_stored{i}") for i in range(2)]
        l0_loaded = [sem(f"l0_loaded{i}") for i in range(2)]
        xa_loaded = [sem(f"xa_loaded{i}") for i in range(2)]
        hb_loaded = [sem(f"hb{n}_loaded") for n in (1, 2)]
        plain_ready = sem("plain_ready")
        plain_used = sem("plain_used")
        split_product = sem("split_product")
        high_ready = sem("high_ready")
        split_ready = sem("split_ready")
        split_used = sem("split_used")
        acc_copied = sem("acc_copied")
        h_copied = sem("h_copied")
        h_stored = [sem(f"h{n}_stored") for n in (1, 2)]
        r01_summed = sem("r01_summed")
        r2_summed = sem("r2_summed")
        mlp1_done = sem("mlp1_done")
        h1_ready = sem("h1_ready")
        mlp2_done = sem("mlp2_done")
        h2_ready = sem("h2_ready")
        mlp3_done = sem("mlp3_done")
        y_ready = sem("y_ready")
        y_stored = sem("y_stored")

        block = ctx.enter_context(nc.Block())

        def loop_chunk(g, j):
            return Chunk(g + j // K, j % K, j // K)

        def loop_step(g, j):
            return [loop_chunk(g, j + ahead) for ahead in (2, 1, 0)]

        def edge_chunk(c):
            return Chunk(c // K, c % K) if 0 <= c < CHUNKS else None

        def edge_step(c):
            return [edge_chunk(x) for x in (c + 2, c + 1, c)]

        AFTER_LOOP = range(K * (GROUPS - 1) + 1, CHUNKS)

        def window(view, steps):
            return bass.AP(view.tensor, view.offset, steps)

        MLP = [(wt1, "wt1"), (wt1d, "wt1d"), (wt2, "wt2"), (wt3, "wt3"), (bt1, "bt1"), (bt2, "bt2"),
               (dense, "dense")]

        def flat(ap):
            return ap.rearrange("p a s -> p (a s)")

        STORES = 4

        def l0_operands(x):
            return (r2[0:ROWS0, 0:2, :], hb[1][0:ROWS0]) if x.edge == 1 else (lx[:], ly[:])

        def hb_of(layer, x):
            if layer == 1 and x.edge == 1:
                return r2
            return hb[0] if x.edge == CHUNKS - 1 else hb[layer - 1]

        raw = [flat((zp[:, 2], zp[:, 1], wt1[:])[layer])[0:ROWS0 if layer == 0 else P, 0:SPLIT_COUNT[layer] * S]
               for layer in range(3)]
        w0b = flat(zp[0:ROWS0, 3])[:, 0:7 * S]

        @block.sync
        def _(sp):
            def load_weights(n):
                sp.dma_start(raw[n], flat(io[f"w{n}"][:, 0:SPLIT_COUNT[n]])).then_inc(w_loaded[n], 16)
                sp.dma_start(wp12[n - 1][:], io[f"w{n}"][:, SPLIT_COUNT[n]:]).then_inc(wp_loaded[n - 1], 16)

            def load_l0(x):
                sp.wait_ge(x_stored[x.k % 2], STORES * 16 * (2 * x.g + x.k // 2 + 1))
                lx, ly = l0_operands(x)
                for c in range(ROT):
                    sp.dma_start(lx[FP * c:FP * (c + 1)],
                                 window(x_rows[x.g, x.k], [[N, FP], [FAR * N, 2], [1, N]])).then_inc(l0_loaded[x.k % 2], 16)
                    sp.dma_start(ly[FP * c:FP * (c + 1)],
                                 window(x_rows[x.g, x.k, c:c + 1], [[N, FP], [ROT * N, 4], [1, N]])
                                 ).then_inc(l0_loaded[x.k % 2], 16)

            def load_xa(x, i):
                sp.dma_start(xa[:, x.k % 2, i], window(x_rows[x.g, x.k, i:i + 1], [[0, RN], [QI * N, QN], [1, N]])
                             ).then_inc(xa_loaded[x.k % 2], 16)

            def load_hb(layer, x):
                sp.wait_ge(h_stored[layer - 1], 16 * (x.c + 1))
                sp.dma_start(hb_of(layer, x)[:], window(h_rows[layer - 1][x.g, x.k],
                                                      [[RJ * N, RN], [0, QN], [1, RJ * N]])
                             ).then_inc(hb_loaded[layer - 1], 16)

            def used(layer, x, op):
                sp.wait_ge(plain_ready, plain_no(layer, x, op) + 1)

            def step(now, after):
                x0, x1, x2 = now
                n0, n1, n2 = after
                if n0:
                    used(0, x0, 0)
                    load_l0(n0)
                if n1:
                    used(1, x1, 2 if n1.edge == 1 else QI - 1)
                    load_hb(1, n1)
                    for op, free in ((2, (0, 2)), (3, (1, 3)), (4, (4,))):
                        if x2:
                            used(2, x2, op)
                        for i in free:
                            load_xa(n1, i)
                if n2:
                    if x2 and n2.edge != CHUNKS - 1:
                        used(2, x2, QI - 1)
                    elif n2.edge == CHUNKS - 1:
                        used(1, x1, QI - 1)
                    load_hb(2, n2)

            c0, c1 = Chunk(0, 0), Chunk(0, 1)
            sp.dma_start(ids[:], io["ids"][0]).then_inc(ids0_loaded, 16)
            sp.dma_start(raw[0], flat(io["w0a"][:, TILES0[0]:])).then_inc(w_loaded[0], 16)
            sp.dma_start(flat(wp0[:]), flat(io["w0a"][:, 0:TILES0[0]])).then_inc(w_loaded[0], 16)
            sp.dma_start(w0b, flat(io["w0b"])).then_inc(w_loaded[0], 16)
            sp.dma_start(bias[:], io["bias"]).then_inc(bias_loaded, 16)
            load_weights(1)
            load_l0(c0)
            for i in range(QI):
                load_xa(c0, i)
            load_l0(c1)
            load_hb(1, c0)
            used(0, c1, 0)
            load_l0(Chunk(0, 2))
            load_weights(2)
            step((None, c0, None), (None, c1, c0))
            step(edge_step(0), edge_step(1))
            sp.wait_ge(w_low, 3)
            for dst, name in MLP:
                sp.dma_start(dst[:] if dst is not dense else dst, io[name]).then_inc(mlp_loaded, 16)
            with sp.Fori(0, GROUPS - 1) as g:
                for j in range(1, K + 1):
                    step(loop_step(g, j), loop_step(g, j + 1))
            for c in AFTER_LOOP:
                step(edge_step(c), edge_step(c + 1))

        @block.gpsimd
        def _(pool):
            def load_ids(g):
                pool.dma_start(ids[:], io["ids"][g]).then_inc(ids_loaded, 16)

            def make_index():
                nc.gpsimd.tensor_tensor(index[:], ids[:], table_start[:].unsqueeze(1).to_broadcast([P, K, GATHERS]),
                                        ALU.add).then_inc(index_ready, 1)

            def gather():
                for k in range(K):
                    for m in range(GATHERS):
                        nc.gpsimd.indirect_dma_start(
                            xg[:, k, m, :], None, io["table"],
                            bass.IndirectOffsetOnAxis(index[:, k, m:m + 1].bitcast(U32), 0)
                        ).then_inc(gathered[k], 16)

            nc.gpsimd.memset(ident[:], 0.0).then_inc(ident_zeroed, 1)
            pool.wait_ge(ident_zeroed, 1)
            nc.gpsimd.affine_select(out=ident[:], in_=ident[:], compare_op=ALU.not_equal, fill=1.0, base=0,
                                    pattern=[[-1, P]], channel_multiplier=1).then_inc(ident_made, 1)
            pool.wait_ge(starts_loaded, 16)
            pool.wait_ge(ids0_loaded, 16)
            make_index()
            pool.wait_ge(index_ready, 1)
            with pool.Fori(0, GROUPS - 1) as g:
                gather()
                load_ids(g + 1)
                for k in range(K):
                    pool.wait_ge(gathered[k], 16 * GATHERS * (g + 1))
                pool.wait_ge(ids_loaded, 16 * (g + 1))
                make_index()
                pool.wait_ge(index_ready, g + 2)
                pool.wait_ge(x_transposed, K * (g + 1))
            gather()

        @block.vector
        def _(dve):
            dve.wait_ge(w_loaded[0], 16 * 3)
            nc.vector.tensor_tensor(raw[0], raw[0], w0b[:, TILES0[0] * S:], ALU.add).then_inc(w0_folded, 1)
            nc.vector.tensor_tensor(flat(wp0[:]), flat(wp0[:]), w0b[:, 0:TILES0[0] * S], ALU.add).then_inc(w0_folded, 1)

            def low_weights(layer):
                rows = ROWS0 if layer == 0 else P
                tiles = slice(SPLIT_TILE[layer], SPLIT_TILE[layer] + SPLIT_COUNT[layer])
                dve.wait_ge(w_high, layer + 1)
                nc.vector.tensor_tensor(flat(ws[0:rows, 1, tiles]), raw[layer],
                                        flat(ws[0:rows, 0, tiles]).bitcast(F32), ALU.subtract).then_inc(w_low, 1)

            def operands(layer, x, op):
                if layer == 0:
                    tiles = TILES0[op]
                    lx, ly = l0_operands(x)
                    return (lx[:, op:op + 1, :].to_broadcast([ROWS0, tiles, N]), ly[:, 4 - tiles:4, :])
                return xa[:, x.k % 2, op:op + 1, :].to_broadcast([P, RJ, N]), hb_of(layer, x)[:]

            def z_slot(ring, n, layer, op=None):
                return ring[0:ROWS0, n, 0:TILES0[op], :] if layer == 0 else ring[:, n]

            def plain(layer, x, op):
                n = plain_no(layer, x, op)
                if x.edge is None or n >= PLAIN_RING:
                    dve.wait_ge(plain_used, n - PLAIN_RING + 1)
                a, b = operands(layer, x, op)
                out = z_slot(zp, plain_no(layer, x.like, op) % PLAIN_RING, layer, op)
                nc.vector.tensor_tensor(out, a, b, ALU.mult).then_inc(plain_ready, 1)

            def split(layer, x, op):
                n = split_no(layer, x, op)
                if x.edge is None or n >= SPLIT_RING:
                    dve.wait_ge(split_ready, n - SPLIT_RING + 1)
                a, b = operands(layer, x, op)
                out = z_slot(zs, split_no(layer, x.like, op) % SPLIT_RING, layer, op)
                nc.vector.tensor_tensor(out, a, b, ALU.mult).then_inc(split_product, 1)

            def low(layer, x, op):
                n = split_no(layer, x.like, op) % SPLIT_RING
                dve.wait_ge(high_ready, split_no(layer, x, op) + 1)
                nc.vector.tensor_tensor(z_slot(zl, n, layer, op), z_slot(zs, n, layer, op),
                                        z_slot(zh, n, layer, op).bitcast(F32), ALU.subtract).then_inc(split_ready, 1)

            def sum_positions(out, r, x, count, done):
                chunks = slice(x.k + 1 - count, x.k + 1)
                nc.vector.tensor_reduce(out[:, chunks], r[:, chunks].rearrange("p k (d b) -> p k b d", b=B), AX.X,
                                        ALU.add).then_inc(done, 1)

            def pair01(x):
                dve.wait_ge(acc_copied, acc_no(1, x) + 1)
                sum_positions(sum01, r01, x, 2, r01_summed)

            def sum_last2(x, count=2):
                dve.wait_ge(acc_copied, acc_no(2, x) + 1)
                sum_positions(sum2, r2, x, count, r2_summed)

            def step(now, odd=False, before2=None):
                x0, x1, x2 = now
                if x0:
                    dve.wait_ge(l0_loaded[x0.k % 2], 16 * 2 * ROT * (2 * x0.g + x0.k // 2 + 1))
                    if x0.edge == 0:
                        plain(0, x0, 0)
                        split(0, x0, 1)
                    else:
                        split(0, x0, 1)
                        plain(0, x0, 0)
                if x0 and x0.edge == 1:
                    low(0, x0, 1)
                if x1:
                    dve.wait_ge(xa_loaded[x1.k % 2], 16 * QI * (2 * x1.g + x1.k // 2 + 1))
                    dve.wait_ge(hb_loaded[0], 16 * (x1.c + 1))
                    split(1, x1, 0)
                if x0 and x0.edge != 1:
                    low(0, x0, 1)
                if odd:
                    pair01(x2)
                if x1:
                    plain(1, x1, 2)
                    split(1, x1, 1)
                    low(1, x1, 0)
                    plain(1, x1, 3)
                    low(1, x1, 1)
                    if before2 and not odd:
                        sum_last2(before2)
                    plain(1, x1, 4)
                if x2 and x2.edge == 0:
                    low_weights(2)
                if x2:
                    dve.wait_ge(hb_loaded[1], 16 * (x2.c + 1))
                    split(2, x2, 0)
                    plain(2, x2, 2)
                    split(2, x2, 1)
                    low(2, x2, 0)
                    plain(2, x2, 3)
                    low(2, x2, 1)
                    plain(2, x2, 4)

            low_weights(0)
            low_weights(1)
            dve.wait_ge(w_low, 2)
            step(edge_step(-2))
            step(edge_step(-1))
            step(edge_step(0))
            with dve.Fori(0, GROUPS - 1) as g:
                for j in range(1, K + 1):
                    step(loop_step(g, j), odd=j % 2 == 1, before2=loop_chunk(g, j - 1))
            for c in AFTER_LOOP:
                step(edge_step(c), odd=c % 2 == 1, before2=edge_chunk(c - 1))
            for c in (CHUNKS - 2, CHUNKS - 1):
                sum_last2(edge_chunk(c), 1)

        @block.tensor
        def _(pe):
            def transpose(x):
                pe.wait_ge(gathered[x.k], 16 * GATHERS * (x.g + 1))
                if x.edge is None or x.edge >= 2:
                    pe.wait_ge(xt_copied, x.c - 1)
                columns = xg[:, x.k].rearrange("p m d -> p (m d)")
                for half in range(2):
                    last = nc.tensor.transpose(xt_ps[x.k % 2][0:HALF, half, :],
                                               columns[:, half * HALF:(half + 1) * HALF], ident[:])
                last.then_inc(x_transposed, 1)

            def layer_ops(layer, x, ops):
                rows = ROWS0 if layer == 0 else P
                a = acc_no(layer, x)
                out = acc[acc_no(layer, x.like) % ACC_RING][:]
                for op in ops:
                    first, final = op == ORDER[layer][0], op == ORDER[layer][-1]
                    if first and (x.edge is None or a >= ACC_RING):
                        pe.wait_ge(acc_copied, a - ACC_RING + 1)
                    tiles = TILES0[op] if layer == 0 else RJ
                    if op in PLAIN_OPS[layer]:
                        pe.wait_ge(plain_ready, plain_no(layer, x, op) + 1)
                        slot = plain_no(layer, x.like, op) % PLAIN_RING
                        w = wp0 if layer == 0 else wp12[layer - 1]
                        t0 = 0 if layer == 0 else RJ * (op - 2)
                        passes = [(w[:, t0 + j, :], zp[0:rows, slot, j, :]) for j in range(tiles)]
                        used = plain_used
                    else:
                        pe.wait_ge(split_ready, split_no(layer, x, op) + 1)
                        slot = split_no(layer, x.like, op) % SPLIT_RING
                        t0 = SPLIT_TILE[layer] + (0 if layer == 0 else RJ * op)
                        passes = []
                        for j in range(tiles):
                            high, low = ws[0:rows, 0, t0 + j, :], ws[0:rows, 1, t0 + j, :]
                            zhj, zlj = zh[0:rows, slot, j, :], zl[0:rows, slot, j, :]
                            passes += [(low, zhj), (high, zlj), (high, zhj)]
                        used = split_used
                    for n, (w, z) in enumerate(passes):
                        last = nc.tensor.matmul(out, w, z, start=(first and n == 0),
                                                stop=(final and n == len(passes) - 1))
                    last.then_inc(used, 1)

            def mlp1(g):
                pe.wait_ge(mlp_loaded, 16 * len(MLP))
                pe.wait_ge(r01_summed, 2 * (g + 1))
                pe.wait_ge(r2_summed, 2 * (g + 1) + (1 if isinstance(g, int) else 0))
                for t in range(T1):
                    m = slice(t * P, (t + 1) * P)
                    nc.tensor.matmul(h1_ps[:, t, :], wt1[:, 0, m], flat(sum01[:]), start=True, stop=False)
                    nc.tensor.matmul(h1_ps[:, t, :], wt1[:, 1, m], flat(sum2[:]), start=False, stop=False)
                    last = nc.tensor.matmul(h1_ps[:, t, :], wt1d[:, m], dense[:, bass.ds(g * P, P)],
                                            start=False, stop=True)
                last.then_inc(mlp1_done, 1)

            def mlp2(g):
                pe.wait_ge(h1_ready, g + 1)
                for t in range(T2):
                    for s in range(T1):
                        last = nc.tensor.matmul(h2_ps[:, t, :], wt2[:, s, t * P:(t + 1) * P], h1[:, s, :],
                                                start=(s == 0), stop=(s == T1 - 1))
                last.then_inc(mlp2_done, 1)

            def mlp3(g):
                pe.wait_ge(h2_ready, g + 1)
                for s in range(T2):
                    last = nc.tensor.matmul(h2_ps[0:1, 2, :], wt3[:, s:s + 1], h2[:, s, :],
                                            start=(s == 0), stop=(s == T2 - 1))
                last.then_inc(mlp3_done, 1)

            def step(now, ahead, group_done=None):
                x0, x1, x2 = now
                early = ahead and ahead.edge == 2
                if early:
                    transpose(ahead)
                if x0:
                    layer_ops(0, x0, ORDER[0])
                if ahead and not early:
                    transpose(ahead)
                if x1:
                    layer_ops(1, x1, ORDER[1])
                if group_done is not None:
                    mlp1(group_done)
                if x2 and x2.edge == 0:
                    pe.wait_ge(w_low, 3)
                    pe.wait_ge(wp_loaded[1], 16)
                if x2:
                    layer_ops(2, x2, ORDER[2][:2])
                    if group_done is not None:
                        mlp2(group_done)
                    layer_ops(2, x2, ORDER[2][2:3])
                    if group_done is not None:
                        mlp3(group_done)
                    layer_ops(2, x2, ORDER[2][3:])

            pe.wait_ge(ident_made, 1)
            transpose(edge_chunk(0))
            transpose(edge_chunk(1))
            pe.wait_ge(w0_folded, 2)
            for c in (-2, -1, 0):
                layer = c + 2
                if layer < 2:
                    pe.wait_ge(w_low, layer + 1)
                if layer == 1:
                    pe.wait_ge(wp_loaded[0], 16)
                step(edge_step(c), edge_chunk(c + 3) if c > -2 else None)
            with pe.Fori(0, GROUPS - 1) as g:
                for j in range(1, K + 1):
                    step(loop_step(g, j), loop_chunk(g, j + 3), group_done=g if j == K else None)
            for c in AFTER_LOOP:
                step(edge_step(c), edge_chunk(c + 3))
            mlp1(GROUPS - 1)
            mlp2(GROUPS - 1)
            mlp3(GROUPS - 1)

        @block.scalar
        def _(act):
            def high(layer, x, op):
                n = split_no(layer, x, op)
                slot = split_no(layer, x.like, op) % SPLIT_RING
                rows, tiles = (ROWS0, TILES0[op]) if layer == 0 else (P, RJ)
                if x.edge is None or n >= SPLIT_RING:
                    act.wait_ge(split_used, n - SPLIT_RING + 1)
                act.wait_ge(split_product, n + 1)
                nc.scalar.copy(zh[0:rows, slot, 0:tiles], zs[0:rows, slot, 0:tiles]).then_inc(high_ready, 1)

            def copy_xt(x):
                if x.edge is None or x.edge >= 2:
                    act.wait_ge(x_stored[x.k % 2], STORES * 16 * (2 * x.g + x.k // 2))
                act.wait_ge(x_transposed, x.c + 1)
                nc.scalar.copy(xt[:, x.k % 2], xt_ps[x.k % 2][0:HALF]).then_inc(xt_copied, 1)
                act.wait_ge(xt_copied, x.c + 1)
                for start, half, es in ((0, 0, E), (0, 1, E), (FP, 0, 3), (FP, 1, 2)):
                    row = start + half * GATHERS // 2
                    act.dma_start(window(x_rows[x.g, x.k, row:row + 1], [[B, HALF], [GATHERS * N, es], [1, B]]),
                                  xt[:, x.k % 2, half, 0:es]).then_inc(x_stored[x.k % 2], 16)

            def relu(out, in_, col):
                rows = slice(out.start_partition(), out.start_partition() + out.shape[0])
                return nc.scalar.activation(out, in_, ACT.Relu, bias=bias[rows, col:col + 1])

            def hidden(layer, x, src, rows):
                n = count_before([1, 1, 0], layer, x)
                relu(hst[rows, :], src[rows, :], layer).then_inc(h_copied, 1)
                act.wait_ge(h_copied, n + 1)
                act.dma_start(h_rows[layer][x.g, x.k], hst[rows, :]).then_inc(h_stored[layer], 16)

            low_rows, high_rows = slice(0, H), slice(H, S)

            def out0(x):
                act.wait_ge(split_used, split_no(0, x, 1) + 1)
                src = acc[acc_no(0, x.like) % ACC_RING]
                if x.edge == 1:
                    act.wait_ge(h_stored[0], 16)
                hidden(0, x, src, low_rows)
                if x.k % 2 == 0 and (x.edge is None or x.edge >= K):
                    act.wait_ge(r01_summed, 2 * x.g + x.k // 2 - 1)
                relu(r01[high_rows, x.k, :], src[high_rows, :], 0).then_inc(acc_copied, 1)

            def out1(x):
                act.wait_ge(plain_used, plain_no(1, x, QI - 1) + 1)
                src = acc[acc_no(1, x.like) % ACC_RING]
                hidden(1, x, src, high_rows)
                relu(r01[low_rows, x.k, :], src[low_rows, :], 1).then_inc(acc_copied, 1)

            def out2(x):
                act.wait_ge(plain_used, plain_no(2, x, QI - 1) + 1)
                relu(r2[:, x.k, :], acc[acc_no(2, x.like) % ACC_RING][:], 2).then_inc(acc_copied, 1)

            def mlp1(g):
                act.wait_ge(mlp_loaded, 16 * len(MLP))
                act.wait_ge(mlp1_done, g + 1)
                for t in range(T1):
                    last = nc.scalar.activation(h1[:, t, :], h1_ps[:, t, :], ACT.Relu, bias=bt1[:, t:t + 1])
                last.then_inc(h1_ready, 1)

            def mlp2(g):
                act.wait_ge(mlp2_done, g + 1)
                for t in range(T2):
                    last = nc.scalar.activation(h2[:, t, :], h2_ps[:, t, :], ACT.Relu, bias=bt2[:, t:t + 1])
                last.then_inc(h2_ready, 1)

            def mlp3(g):
                act.wait_ge(mlp3_done, g + 1)
                nc.scalar.copy(y[:, bass.ds(g * P, P)], h2_ps[0:1, 2, :]).then_inc(y_ready, 1)

            def step(now, ahead, before2=None, group_done=None):
                x0, x1, x2 = now
                early = ahead and ahead.edge == 2
                if early:
                    copy_xt(ahead)
                if x0:
                    high(0, x0, 1)
                if early:
                    out0(x0)
                if x2 and x2.edge == 0:
                    out1(x2)
                if x1:
                    high(1, x1, 0)
                if before2:
                    out2(before2)
                if x1:
                    high(1, x1, 1)
                if early:
                    high_weights(2)
                if x0 and not early:
                    out0(x0)
                if ahead and not early:
                    copy_xt(ahead)
                if x2:
                    high(2, x2, 0)
                    high(2, x2, 1)
                if x1 and x1.edge != 0:
                    out1(x1)
                if group_done is not None:
                    mlp1(group_done)
                    mlp2(group_done)
                    mlp3(group_done)

            def high_weights(layer):
                rows = ROWS0 if layer == 0 else P
                tiles = slice(SPLIT_TILE[layer], SPLIT_TILE[layer] + SPLIT_COUNT[layer])
                if layer == 0:
                    act.wait_ge(w0_folded, 1)
                else:
                    act.wait_ge(w_loaded[layer], 16)
                nc.scalar.copy(flat(ws[0:rows, 0, tiles]), raw[layer]).then_inc(w_high, 1)

            act.dma_start(table_start[:], io["table_start"]).then_inc(starts_loaded, 16)
            high_weights(0)
            high_weights(1)
            act.wait_ge(bias_loaded, 16)
            copy_xt(edge_chunk(0))
            copy_xt(edge_chunk(1))
            step(edge_step(-2), None)
            step(edge_step(-1), edge_chunk(2))
            step(edge_step(0), edge_chunk(3))
            with act.Fori(0, GROUPS - 1) as g:
                for j in range(1, K + 1):
                    step(loop_step(g, j), loop_chunk(g, j + 3), loop_chunk(g, j - 1),
                         group_done=g if j == K else None)
            for c in AFTER_LOOP:
                step(edge_step(c), edge_chunk(c + 3), edge_chunk(c - 1))
            out2(edge_chunk(CHUNKS - 1))
            mlp1(GROUPS - 1)
            mlp2(GROUPS - 1)
            mlp3(GROUPS - 1)
            act.wait_ge(y_ready, GROUPS)
            act.dma_start(io["out"], y).then_inc(y_stored, 16)
            act.wait_ge(y_stored, 16)


def tile_rows0(W):
    Wp = np.zeros((FP, FP, S), W.dtype)
    Wp[:FIELDS, :FIELDS] = W.reshape(FIELDS, FIELDS, S)
    ab, ba = np.zeros((2, ROWS0, sum(TILES0), S), W.dtype)
    t = 0
    for u, tiles in enumerate(TILES0):
        for v in range(4 - tiles, 4):
            for c in range(ROT):
                for f in range(FP):
                    a, b = (f + FAR * u) % FP, (f + ROT * v + c) % FP
                    ab[FP * c + f, t] = Wp[a, b]
                    if (a - b) % FP not in (0, FP // 2):
                        ba[FP * c + f, t] = Wp[b, a]
            t += 1
    return ab, ba


def tile_rows12(W, maps):
    Wp = np.zeros((QN * QI, H, S), W.dtype)
    Wp[:FIELDS] = W.reshape(FIELDS, H, S)[:, :, maps]
    return Wp.reshape(QN, QI, RN, RJ, S).transpose(2, 0, 1, 3, 4).reshape(P, PAIR_TILES, S)


def kernel(**inputs):
    import concourse.bacc as bacc
    from concourse.bass_utils import run_bass_kernel_spmd

    a = {name: np.asarray(v) for name, v in inputs.items()}
    direct_first = np.r_[H:S, 0:H]
    w0a, w0b = tile_rows0(a["L0_rec_W0"])
    top1 = a["W_top1"]
    tables = [a[f"tbl_{f}"] for f in range(FIELDS)]
    starts = np.cumsum([0, *(len(t) for t in tables)]).astype(np.int32)
    arrays = {
        "ids": np.pad(a["ids"], ((0, 0), (0, FP - FIELDS))).reshape(GROUPS, K, B, E, GATHERS)
                 .transpose(0, 3, 2, 1, 4).reshape(GROUPS, P, K, GATHERS),
        "table_start": np.repeat(starts.reshape(E, GATHERS), B, axis=0),
        "table": np.concatenate([*tables, np.zeros((1, D), tables[0].dtype)]),
        "w0a": w0a, "w0b": w0b,
        "w1": tile_rows12(a["L0_rec_W1"], direct_first),
        "w2": tile_rows12(a["L0_rec_W2"], np.arange(S)),
        "wt1": np.stack([np.concatenate([top1[H:S], top1[0:H]]), top1[S:2 * S]], axis=1),
        "wt1d": top1[2 * S:],
        "wt2": a["W_top2"].reshape(T1, P, M2).transpose(1, 0, 2),
        "wt3": a["W_top3"].reshape(T2, P).T,
        "bias": np.stack([a["L0_rec_b0"], a["L0_rec_b1"][direct_first], a["L0_rec_b2"]], axis=1),
        "bt1": a["b_top1"].reshape(T1, P).T,
        "bt2": a["b_top2"].reshape(T2, P).T,
        "dense": a["dense_ctx"].T,
    }
    arrays = {name: np.ascontiguousarray(v) for name, v in arrays.items()}

    nc = bacc.Bacc("TRN2", target_bir_lowering=False, num_devices=1)
    io = {name: nc.dram_tensor("in_" + name, v.shape, mybir.dt.from_np(v.dtype), kind="ExternalInput").ap()
          for name, v in arrays.items()}
    io["out"] = nc.dram_tensor("out_y", (1, BATCH), F32, kind="ExternalOutput").ap()
    build(nc, io)
    r = run_bass_kernel_spmd(nc, [{"in_" + name: v for name, v in arrays.items()}], core_ids=[0])
    return r.results[0]["out_y"].reshape(BATCH, 1)
```
